# Optimizing a Trainium2 kernel written in Bass

```python
import numpy as np
import jax
import jax.numpy as jnp

def _softmax(x, axis=-1):
    return jax.nn.softmax(x, axis=axis)
def _gelu(x):
    return jax.nn.gelu(x, approximate=True)
def _silu(x):
    return jax.nn.silu(x)
def _sigmoid(x):
    return jax.nn.sigmoid(x)
def _layernorm(x, axis=-1, eps=1e-5):
    m = jnp.mean(x, axis=axis, keepdims=True)
    v = jnp.var(x, axis=axis, keepdims=True)
    return (x - m) / jnp.sqrt(v + eps)
def _scatter_add(tgt, idx, src, axis=0):
    return tgt.at[idx].add(src)
def _segment_sum(src, seg, n):
    return jax.ops.segment_sum(src, seg, n)

kernel_name = 'mk_conv_preact_d2_conv_nchw512_c30eed'

def setup_inputs(seed: int = 0):
    np.random.seed(seed)
    _w = jnp.asarray
    def _rec_inputs():
        import jax
        import jax.numpy as jnp
        _gk = jax.random.key(seed)
        x = -8.268e-05 + 0.9999 * jax.random.normal(jax.random.fold_in(_gk, 1), (32, 512, 56, 56), jnp.float32)
        return x
    x = _rec_inputs()
    def _L0_conv_setup():
        import jax, jax.numpy as jnp
        import numpy as np
        from jax import lax
        B, C, H, W = (32, 512, 56, 56)
        HN = 16
        HD = C // HN
        GC = C // 4
        KS = [3, 5, 7, 9]
        WIN = 7
        EPS = 1e-05

        def _dwconv1d(x, w, b, k):
            y = lax.conv_general_dilated(x, w, window_strides=(1,), padding=[(k // 2, k // 2)], dimension_numbers=('NCH', 'OIH', 'NCH'), feature_group_count=x.shape[1])
            return y + b[None, :, None]

        def _group_norm(x, gamma, beta, groups):
            b, c = (x.shape[0], x.shape[1])
            xr = x.reshape(b, groups, -1)
            mu = xr.mean(-1, keepdims=True)
            var = xr.var(-1, keepdims=True)
            xn = ((xr - mu) * lax.rsqrt(var + EPS)).reshape(x.shape)
            gs = (1, c) + (1,) * (x.ndim - 2)
            return xn * gamma.reshape(gs) + beta.reshape(gs)

        def _forward(x, w_lh, b_lh, w_sh, b_sh, w_mh, b_mh, w_gh, b_gh, w_lw, b_lw, w_sw, b_sw, w_mw, b_mw, w_gw, b_gw, gn_h_g, gn_h_b, gn_w_g, gn_w_b, gn_g, gn_b, wq, wk, wv):
            x_h = x.mean(3)
            x_w = x.mean(2)

            def branch(xs, ws, bs):
                outs = [_dwconv1d(xs[:, i * GC:(i + 1) * GC], w, b, k) for i, (w, b, k) in enumerate(zip(ws, bs, KS))]
                return jnp.concatenate(outs, axis=1)
            h_feat = branch(x_h, (w_lh, w_sh, w_mh, w_gh), (b_lh, b_sh, b_mh, b_gh))
            w_feat = branch(x_w, (w_lw, w_sw, w_mw, w_gw), (b_lw, b_sw, b_mw, b_gw))
            x_h_attn = jax.nn.sigmoid(_group_norm(h_feat, gn_h_g, gn_h_b, 4))
            x_w_attn = jax.nn.sigmoid(_group_norm(w_feat, gn_w_g, gn_w_b, 4))
            xg = x * x_h_attn[:, :, :, None] * x_w_attn[:, :, None, :]
            y = lax.reduce_window(xg, -jnp.inf, lax.max, (1, 1, WIN, WIN), (1, 1, WIN, WIN), 'VALID')
            y = _group_norm(y, gn_g, gn_b, 1)
            hp, wp = (y.shape[2], y.shape[3])
            q = (y * wq[None, :, None, None]).reshape(B, HN, HD, hp * wp)
            k = (y * wk[None, :, None, None]).reshape(B, HN, HD, hp * wp)
            v = (y * wv[None, :, None, None]).reshape(B, HN, HD, hp * wp)
            attn = jnp.einsum('bnil,bnjl->bnij', q, k) * HD ** (-0.5)
            attn = jax.nn.softmax(attn, axis=-1)
            o = jnp.einsum('bnij,bnjl->bnil', attn, v).reshape(B, C, hp, wp)
            ca = jax.nn.sigmoid(o.mean((2, 3), keepdims=True))
            return ca * xg
        key = jax.random.key(seed)
        ks = jax.random.split(key, 20)
        d = {'x': jax.random.normal(ks[0], (B, C, H, W), jnp.float32)}
        names = ['lh', 'sh', 'mh', 'gh', 'lw', 'sw', 'mw', 'gw']
        kers = KS + KS
        for i, nm in enumerate(names):
            d['w_' + nm] = jax.random.normal(ks[1 + i], (GC, 1, kers[i]), jnp.float32) * 0.1
            d['b_' + nm] = jnp.zeros((GC,), jnp.float32)
        for nm in ('gn_h', 'gn_w', 'gn'):
            d[nm + '_g'] = jnp.ones((C,), jnp.float32)
            d[nm + '_b'] = jnp.zeros((C,), jnp.float32)
        d['wq'] = jax.random.normal(ks[10], (C,), jnp.float32) * 0.1
        d['wk'] = jax.random.normal(ks[11], (C,), jnp.float32) * 0.1
        d['wv'] = jax.random.normal(ks[12], (C,), jnp.float32) * 0.1
        return d
    _L0_conv_all = _L0_conv_setup()
    _L0_conv_in = {k: v for k, v in _L0_conv_all.items() if k in ('w_lh', 'b_lh', 'w_sh', 'b_sh', 'w_mh', 'b_mh', 'w_gh', 'b_gh', 'w_lw', 'b_lw', 'w_sw', 'b_sw', 'w_mw', 'b_mw', 'w_gw', 'b_gw', 'gn_h_g', 'gn_h_b', 'gn_w_g', 'gn_w_b', 'gn_g', 'gn_b', 'wq', 'wk', 'wv', )}
    del _L0_conv_all

    def _L1_conv_setup():
        import jax, jax.numpy as jnp
        import numpy as np
        WS = 8
        SHIFT = 4
        HEADS = 16
        key = jax.random.key(seed)
        k1, k2, k3 = jax.random.split(key, 3)
        x = jax.random.normal(k1, (16, 512, 128, 128), dtype=jnp.float32)
        w = jax.random.normal(k2, (HEADS, WS * WS, WS * WS), dtype=jnp.float32) * 0.02
        b = jax.random.normal(k3, (HEADS, WS * WS), dtype=jnp.float32) * 0.02
        return {'x': x, 'w': w, 'b': b}
    _L1_conv_all = _L1_conv_setup()
    _L1_conv_in = {k: v for k, v in _L1_conv_all.items() if k in ('w', 'b', )}
    del _L1_conv_all

    return {
        "x": x,
        "L0_conv_w_lh": _L0_conv_in["w_lh"],
        "L0_conv_b_lh": _L0_conv_in["b_lh"],
        "L0_conv_w_sh": _L0_conv_in["w_sh"],
        "L0_conv_b_sh": _L0_conv_in["b_sh"],
        "L0_conv_w_mh": _L0_conv_in["w_mh"],
        "L0_conv_b_mh": _L0_conv_in["b_mh"],
        "L0_conv_w_gh": _L0_conv_in["w_gh"],
        "L0_conv_b_gh": _L0_conv_in["b_gh"],
        "L0_conv_w_lw": _L0_conv_in["w_lw"],
        "L0_conv_b_lw": _L0_conv_in["b_lw"],
        "L0_conv_w_sw": _L0_conv_in["w_sw"],
        "L0_conv_b_sw": _L0_conv_in["b_sw"],
        "L0_conv_w_mw": _L0_conv_in["w_mw"],
        "L0_conv_b_mw": _L0_conv_in["b_mw"],
        "L0_conv_w_gw": _L0_conv_in["w_gw"],
        "L0_conv_b_gw": _L0_conv_in["b_gw"],
        "L0_conv_gn_h_g": _L0_conv_in["gn_h_g"],
        "L0_conv_gn_h_b": _L0_conv_in["gn_h_b"],
        "L0_conv_gn_w_g": _L0_conv_in["gn_w_g"],
        "L0_conv_gn_w_b": _L0_conv_in["gn_w_b"],
        "L0_conv_gn_g": _L0_conv_in["gn_g"],
        "L0_conv_gn_b": _L0_conv_in["gn_b"],
        "L0_conv_wq": _L0_conv_in["wq"],
        "L0_conv_wk": _L0_conv_in["wk"],
        "L0_conv_wv": _L0_conv_in["wv"],
        "L1_conv_w": _L1_conv_in["w"],
        "L1_conv_b": _L1_conv_in["b"],
    }

def reference(x, L0_conv_w_lh, L0_conv_b_lh, L0_conv_w_sh, L0_conv_b_sh, L0_conv_w_mh, L0_conv_b_mh, L0_conv_w_gh, L0_conv_b_gh, L0_conv_w_lw, L0_conv_b_lw, L0_conv_w_sw, L0_conv_b_sw, L0_conv_w_mw, L0_conv_b_mw, L0_conv_w_gw, L0_conv_b_gw, L0_conv_gn_h_g, L0_conv_gn_h_b, L0_conv_gn_w_g, L0_conv_gn_w_b, L0_conv_gn_g, L0_conv_gn_b, L0_conv_wq, L0_conv_wk, L0_conv_wv, L1_conv_w, L1_conv_b):
    import jax
    import jax.numpy as jnp
    def _L0_conv_ref(x, w_lh, b_lh, w_sh, b_sh, w_mh, b_mh, w_gh, b_gh, w_lw, b_lw, w_sw, b_sw, w_mw, b_mw, w_gw, b_gw, gn_h_g, gn_h_b, gn_w_g, gn_w_b, gn_g, gn_b, wq, wk, wv):
        import jax, jax.numpy as jnp
        import numpy as np
        from jax import lax
        B, C, H, W = (32, 512, 56, 56)
        HN = 16
        HD = C // HN
        GC = C // 4
        KS = [3, 5, 7, 9]
        WIN = 7
        EPS = 1e-05

        def _dwconv1d(x, w, b, k):
            y = lax.conv_general_dilated(x, w, window_strides=(1,), padding=[(k // 2, k // 2)], dimension_numbers=('NCH', 'OIH', 'NCH'), feature_group_count=x.shape[1])
            return y + b[None, :, None]

        def _group_norm(x, gamma, beta, groups):
            b, c = (x.shape[0], x.shape[1])
            xr = x.reshape(b, groups, -1)
            mu = xr.mean(-1, keepdims=True)
            var = xr.var(-1, keepdims=True)
            xn = ((xr - mu) * lax.rsqrt(var + EPS)).reshape(x.shape)
            gs = (1, c) + (1,) * (x.ndim - 2)
            return xn * gamma.reshape(gs) + beta.reshape(gs)

        def _forward(x, w_lh, b_lh, w_sh, b_sh, w_mh, b_mh, w_gh, b_gh, w_lw, b_lw, w_sw, b_sw, w_mw, b_mw, w_gw, b_gw, gn_h_g, gn_h_b, gn_w_g, gn_w_b, gn_g, gn_b, wq, wk, wv):
            x_h = x.mean(3)
            x_w = x.mean(2)

            def branch(xs, ws, bs):
                outs = [_dwconv1d(xs[:, i * GC:(i + 1) * GC], w, b, k) for i, (w, b, k) in enumerate(zip(ws, bs, KS))]
                return jnp.concatenate(outs, axis=1)
            h_feat = branch(x_h, (w_lh, w_sh, w_mh, w_gh), (b_lh, b_sh, b_mh, b_gh))
            w_feat = branch(x_w, (w_lw, w_sw, w_mw, w_gw), (b_lw, b_sw, b_mw, b_gw))
            x_h_attn = jax.nn.sigmoid(_group_norm(h_feat, gn_h_g, gn_h_b, 4))
            x_w_attn = jax.nn.sigmoid(_group_norm(w_feat, gn_w_g, gn_w_b, 4))
            xg = x * x_h_attn[:, :, :, None] * x_w_attn[:, :, None, :]
            y = lax.reduce_window(xg, -jnp.inf, lax.max, (1, 1, WIN, WIN), (1, 1, WIN, WIN), 'VALID')
            y = _group_norm(y, gn_g, gn_b, 1)
            hp, wp = (y.shape[2], y.shape[3])
            q = (y * wq[None, :, None, None]).reshape(B, HN, HD, hp * wp)
            k = (y * wk[None, :, None, None]).reshape(B, HN, HD, hp * wp)
            v = (y * wv[None, :, None, None]).reshape(B, HN, HD, hp * wp)
            attn = jnp.einsum('bnil,bnjl->bnij', q, k) * HD ** (-0.5)
            attn = jax.nn.softmax(attn, axis=-1)
            o = jnp.einsum('bnij,bnjl->bnil', attn, v).reshape(B, C, hp, wp)
            ca = jax.nn.sigmoid(o.mean((2, 3), keepdims=True))
            return ca * xg
        return _forward(x, w_lh, b_lh, w_sh, b_sh, w_mh, b_mh, w_gh, b_gh, w_lw, b_lw, w_sw, b_sw, w_mw, b_mw, w_gw, b_gw, gn_h_g, gn_h_b, gn_w_g, gn_w_b, gn_g, gn_b, wq, wk, wv)

    def _L1_conv_ref(x, w, b):
        import jax, jax.numpy as jnp
        import numpy as np
        WS = 8
        SHIFT = 4
        HEADS = 16
        ws, shift, heads = (WS, SHIFT, HEADS)
        B, C, H, W = x.shape
        hd = C // heads
        ws2 = ws * ws
        x = jnp.transpose(x, (0, 2, 3, 1))
        Pl, Pr, Pt, Pb = (ws - shift, shift, ws - shift, shift)
        x = jnp.pad(x, ((0, 0), (Pt, Pb), (Pl, Pr), (0, 0)))
        _H, _W = (H + ws, W + ws)
        nWh, nWw = (_H // ws, _W // ws)
        xw = x.reshape(B, nWh, ws, nWw, ws, C)
        xw = jnp.transpose(xw, (0, 1, 3, 2, 4, 5)).reshape(-1, ws2, heads, hd)
        xw = jnp.transpose(xw, (0, 2, 1, 3))
        y = jnp.einsum('nhjd,hij->nhid', xw, w) + b[None, :, :, None]
        y = jnp.transpose(y, (0, 2, 1, 3)).reshape(-1, ws, ws, C)
        y = y.reshape(B, nWh, nWw, ws, ws, C)
        y = jnp.transpose(y, (0, 1, 3, 2, 4, 5)).reshape(B, _H, _W, C)
        y = y[:, Pt:_H - Pb, Pl:_W - Pr, :]
        return jnp.transpose(y, (0, 3, 1, 2))

    def _gn(v, G=32, eps=1e-5):
        B_, C_, H_, W_ = v.shape
        g = v.reshape(B_, G, C_ // G, H_, W_)
        m = jnp.mean(g, axis=(2, 3, 4), keepdims=True)
        s = jnp.var(g, axis=(2, 3, 4), keepdims=True)
        return ((g - m) / jnp.sqrt(s + eps)).reshape(v.shape)

    def _ln_c(v, eps=1e-6):
        m = jnp.mean(v, axis=1, keepdims=True)
        s = jnp.var(v, axis=1, keepdims=True)
        return (v - m) / jnp.sqrt(s + eps)

    def _ln_t(v, eps=1e-5):
        m = jnp.mean(v, axis=-1, keepdims=True)
        s = jnp.var(v, axis=-1, keepdims=True)
        return (v - m) / jnp.sqrt(s + eps)

    def _to_tokens(v):
        B_, C_, H_, W_ = v.shape
        return v.reshape(B_, C_, H_ * W_).transpose(0, 2, 1)
    def _from_tokens(t, like):
        B_, C_, H_, W_ = like.shape
        return t.transpose(0, 2, 1).reshape(B_, C_, H_, W_)

    x = x + _L0_conv_ref(_gn(x), L0_conv_w_lh, L0_conv_b_lh, L0_conv_w_sh, L0_conv_b_sh, L0_conv_w_mh, L0_conv_b_mh, L0_conv_w_gh, L0_conv_b_gh, L0_conv_w_lw, L0_conv_b_lw, L0_conv_w_sw, L0_conv_b_sw, L0_conv_w_mw, L0_conv_b_mw, L0_conv_w_gw, L0_conv_b_gw, L0_conv_gn_h_g, L0_conv_gn_h_b, L0_conv_gn_w_g, L0_conv_gn_w_b, L0_conv_gn_g, L0_conv_gn_b, L0_conv_wq, L0_conv_wk, L0_conv_wv)
    x = x + _L1_conv_ref(_gn(x), L1_conv_w, L1_conv_b)
    return x


_drawn_inputs = setup_inputs


def setup_inputs(seed=0):
    import zlib

    import numpy as np

    out = dict(_drawn_inputs(seed))
    spreads = {'L0_conv_b_lh': (0.0, 0.271),
     'L0_conv_b_sh': (0.0, 0.336),
     'L0_conv_b_mh': (0.0, 0.365),
     'L0_conv_b_gh': (0.0, 0.275),
     'L0_conv_b_lw': (0.0, 0.1),
     'L0_conv_b_sw': (0.0, 0.306),
     'L0_conv_b_mw': (0.0, 0.272),
     'L0_conv_b_gw': (0.0, 0.284),
     'L0_conv_gn_h_g': (1.0, 0.6),
     'L0_conv_gn_h_b': (0.0, 0.8),
     'L0_conv_gn_w_g': (1.0, 0.6),
     'L0_conv_gn_w_b': (0.0, 0.8),
     'L0_conv_gn_g': (1.0, 0.6),
     'L0_conv_gn_b': (0.0, 0.8)}
    factors = {'L0_conv_w_lh': 8.0,
     'L0_conv_w_sh': 7.658,
     'L0_conv_w_mh': 6.554,
     'L0_conv_w_gh': 6.641,
     'L0_conv_w_lw': 8.0,
     'L0_conv_w_sw': 7.61,
     'L0_conv_w_mw': 7.049,
     'L0_conv_w_gw': 5.735,
     'L0_conv_wq': 8.0,
     'L0_conv_wk': 8.0,
     'L0_conv_wv': 8.0,
     'L1_conv_b': 3.158}
    for name, (base, spread) in spreads.items():
        noise = np.random.default_rng([zlib.crc32(name.encode()), seed]).standard_normal(out[name].shape)
        drawn = base * np.exp(spread * noise) if base else spread * noise
        out[name] = jnp.asarray(drawn.astype(out[name].dtype))
    for name, factor in factors.items():
        out[name] = (out[name] * factor).astype(out[name].dtype)
    return out
```

```python
import numpy as np
from contextlib import ExitStack

import concourse.bass as bass
from concourse import mybir

F32 = mybir.dt.float32
BF16 = mybir.dt.bfloat16
ALU = mybir.AluOpType
ACT = mybir.ActivationFunctionType
AX = mybir.AxisListType

B, C, H, W = 32, 512, 56, 56
P = 128
T = C // P
HW = H * W
KS = (3, 5, 7, 9)
NTAPS = sum(KS)
PADW = 64
PAD = 4
WIN = 7
NW = H // WIN
L = NW * NW
HEADS, HD = 16, 32
HPT = P // HD
WS, SHIFT = 8, 4
KINDS = 4
INTERIOR, SIDES, ENDS, CORNERS = range(KINDS)
COLS = 6
UNITS = COLS + 2
IN = H - 2 * SHIFT
NB3 = 3 * P
XT_SLOTS = 3
XP_BANKS = 2
Y_BANKS = 2
GROUP = 16
EPS = 1e-5


def block_positions(kind):
    out = []
    for w in range(2 if kind != CORNERS else 1):
        if kind == INTERIOR:
            out += [(w, r * WS + c) for r in range(WS) for c in range(WS)]
        elif kind == SIDES:
            out += [(2 * w + side, r * WS + SHIFT * (1 - side) + c)
                    for r in range(WS) for side in range(2) for c in range(SHIFT)]
        elif kind == ENDS:
            out += [(2 * w + end, (SHIFT * (1 - end) + r) * WS + c)
                    for end in range(2) for r in range(SHIFT) for c in range(WS)]
        else:
            out += [(2 * end + side, (SHIFT * (1 - end) + r) * WS + SHIFT * (1 - side) + c)
                    for end in range(2) for r in range(SHIFT) for side in range(2) for c in range(SHIFT)]
    return out


def build(nc, x, w_conv, b_conv, gam, wk, wv, w_win, b_win, ident_d, gmean_d, heads_d, out):
    with ExitStack() as ctx:
        def sb(name, shape, dt=F32):
            return ctx.enter_context(nc.sbuf_tensor(name, shape, dt))

        def pb(name):
            return ctx.enter_context(nc.psum_tensor(name, [P, 512], F32))

        def sem(name):
            return ctx.enter_context(nc.semaphore(name))

        ident = sb("ident", [P, P])
        gmean = sb("gmean", [P, P])
        ones_h = sb("ones_h", [P, P])
        ones_l = sb("ones_l", [L, HD])
        heads = sb("heads", [P, T, P], BF16)
        bpat = sb("bpat", [P, KINDS, P], BF16)
        wwin = sb("wwin", [P, KINDS - 1, HEADS, P])
        wcor = sb("wcor", [2 * HD, HEADS, 2 * HD])
        wc = sb("wc", [P, 2, NTAPS])
        bc = sb("bc", [P, 2, T])
        gmb = sb("gmb", [P, 7, T])
        wqk_s = sb("wqk_s", [P, T, HD])
        wv_s = sb("wv_s", [P, T, HD])
        eps_s = sb("eps_s", [P, 1])
        mhalf = sb("mhalf", [P, 8])
        xs = sb("xs", [P, 2, T, HW])
        ub = sb("ub", [P, T, HW])
        spare = sb("spare", [P, HW // 2])
        junk = spare[:, :].bitcast(BF16)
        ynt = spare[0:L, 0:C]
        yj = spare[:, C:C + T * L]
        xt = sb("xt", [P, XT_SLOTS, 4 * P])
        rs = sb("rs", [P, 2, T, H])
        chs = sb("chs", [P, T])
        nm1 = sb("nm1", [P, T])
        sq1 = sb("sq1", [P, T])
        ve1 = sb("ve1", [P, T])
        r1 = sb("r1", [P, T])
        xp = sb("xp", [P, 2, T, PADW])
        ff = sb("ff", [P, 2, 2, T, H])
        fs = sb("fs", [P, 16])
        fm = sb("fm", [P, 16])
        hv = sb("hv", [P, 4, 8])
        rh = sb("rh", [P, 8])
        th = sb("th", [P, 2, T, H])
        pm = sb("pm", [P, H * NW])
        y = sb("y", [P, T, L])
        ys = sb("ys", [P, 2])
        ym = sb("ym", [P, 2])
        yv = sb("yv", [P, 2])
        ry = sb("ry", [P, 1])
        ab = sb("ab", [P, 3, T])
        at = sb("at", [P, T, HD])
        mx = sb("mx", [P, T])
        ee = sb("ee", [P, 2, T, HD])
        ss = sb("ss", [P, 2, T])
        rd = sb("rd", [P, T])
        oo = sb("oo", [P, T])
        tc = sb("tc", [P, T])
        ca = sb("ca", [P, T])
        s2 = sb("s2", [P, T])
        nm2 = sb("nm2", [P, T])
        sq2 = sb("sq2", [P, T])
        ve2 = sb("ve2", [P, T])
        r2 = sb("r2", [P, T])
        nmr2 = sb("nmr2", [P, T])

        p_xt = [pb(f"p_xt{i}") for i in range(XP_BANKS)]
        p_y = [pb(f"p_y{i}") for i in range(Y_BANKS)]
        p_col = [pb(f"p_col{i}") for i in range(2)]
        p_front, p_back = pb("p_front"), pb("p_back")
        p_gram, p_vb = p_col[1][:, 0:P], p_col[1][:, P:2 * P]
        p_m1, p_v1, p_fm, p_ym = p_front[:, 0:4], p_front[:, 8:12], p_front[:, 16:32], p_front[:, 32:34]
        p_m2, p_v2 = p_back[:, 0:4], p_back[:, 8:12]

        consts_in, wwin_in, b_in = sem("consts_in"), sem("wwin_in"), sem("b_in")
        psum_clear, zeros_set, consts_set = sem("psum_clear"), sem("zeros_set"), sem("consts_set")
        split = sem("split")
        x_in = [sem(f"x_in{t}") for t in range(T)]
        out_done = [sem(f"out_done{t}") for t in range(T)]
        rowsum_done, colsum_ready, colsum_read, chsum_done = (
            sem("rowsum_done"), sem("colsum_ready"), sem("colsum_read"), sem("chsum_done"))
        m1_ready, nm1_done, sq1_done, v1_ready, ve1_done, r1_done = (
            sem("m1_ready"), sem("nm1_done"), sem("sq1_done"), sem("v1_ready"), sem("ve1_done"), sem("r1_done"))
        centred, tap_done, f_done, fstat_done = sem("centred"), sem("tap_done"), sem("f_done"), sem("fstat_done")
        fm_ready, fm_done, vh_done, rh_done, hb_done, th_done, gate_done = (
            sem("fm_ready"), sem("fm_done"), sem("vh_done"), sem("rh_done"), sem("hb_done"), sem("th_done"),
            sem("gate_done"))
        u_done, wmax_done, wgate_done, y_done, v_done = (
            sem("u_done"), sem("wmax_done"), sem("wgate_done"), sem("y_done"), sem("v_done"))
        ystat_done, ym_ready, ym_done, yvar_done, ry_done, yn_done = (
            sem("ystat_done"), sem("ym_ready"), sem("ym_done"), sem("yvar_done"), sem("ry_done"), sem("yn_done"))
        ynt_ready, ynt_done, gram_ready, att_done, exp_done, tc_done, ca_done, x1_done = (
            sem("ynt_ready"), sem("ynt_done"), sem("gram_ready"), sem("att_done"), sem("exp_done"), sem("tc_done"),
            sem("ca_done"), sem("x1_done"))
        m2_ready, nm2_done, sq2_done, v2_ready, ve2_done, r2_done, nmr2_done, xn_done = (
            sem("m2_ready"), sem("nm2_done"), sem("sq2_done"), sem("v2_ready"), sem("ve2_done"), sem("r2_done"),
            sem("nmr2_done"), sem("xn_done"))
        passed_pool, passed_pe = sem("passed_pool"), sem("passed_pe")
        gv, yq, rdone = sem("gate_var_step"), sem("pooled_norm_step"), sem("recip_done")
        xt_ready, xt_copied, mix_ready, added = sem("xt_ready"), sem("xt_copied"), sem("mix_ready"), sem("added")

        block = ctx.enter_context(nc.Block())

        TAPS2 = 2 * NTAPS
        ATT = 7
        XN = 6
        F3 = 4
        HB = 3
        BACK = UNITS * T

        def freed(n, k, places):
            return (n - 1) * BACK + (k - places + 1 if k >= places else 0)

        def wait(eng, s, value):
            if not (isinstance(value, int) and value <= 0):
                eng.wait_ge(s, value)

        def image(ap):
            return ap.rearrange("p (h w) -> p h w", w=W)

        def kind_of(j):
            return INTERIOR if j < COLS else (SIDES if j == COLS else ENDS)

        def image_pieces(t_map):
            m = image(t_map)
            ends = m.rearrange("p (e r) w -> p e r w", r=SHIFT)
            mid = m[:, SHIFT:SHIFT + IN, :]
            return ([mid[:, :, SHIFT:SHIFT + IN].rearrange("p h (k c) -> p k h c", c=WS),
                     mid.rearrange("p h (s c) -> p h s c", c=SHIFT)[:, :, 0:14:13, :]]
                    + [ends[:, 13 * e, :, SHIFT:SHIFT + IN].rearrange("p r (k c) -> p k r c", c=WS) for e in range(2)]
                    + [ends[:, 13 * e].rearrange("p r (s c) -> p r s c", c=SHIFT)[:, :, 0:14:13, :] for e in range(2)])

        def sides_in(unit):
            return [unit[:, 0:NB3].rearrange("p (h s c) -> p h s c", s=2, c=SHIFT)]

        def ends_in(unit):
            e4 = unit[:, 0:NB3].rearrange("p (k e r c) -> p e k r c", e=2, r=SHIFT, c=WS)
            c4 = unit[:, NB3:NB3 + 64].rearrange("p (e r s c) -> p e r s c", e=2, r=SHIFT, s=2)
            return [e4[:, 0], e4[:, 1], c4[:, 0], c4[:, 1]]

        @block.sync
        def _(sp):
            for dst, src in ((ident[:, :], ident_d), (gmean[:, :], gmean_d), (wc[:, :, :], w_conv), (bc[:, :, :], b_conv),
                             (gmb[:, :, :], gam)):
                sp.dma_start(dst, src).then_inc(consts_in, 16)
            for q in range(HPT):
                rows = slice(HD * q, HD * (q + 1))
                wk_v = wk.rearrange("(t q c) -> q t c", q=HPT, c=HD)[q:q + 1].broadcast_to([HD, T, HD])
                wv_v = wv.rearrange("(t q c) -> q t c", q=HPT, c=HD)[q:q + 1].broadcast_to([HD, T, HD])
                sp.dma_start(wqk_s[rows, :, :], wk_v).then_inc(consts_in, 16)
                sp.dma_start(wv_s[rows, :, :], wv_v).then_inc(consts_in, 16)
            sp.wait_ge(zeros_set, 1)
            for part in range(3):
                sp.dma_start(ub[32 * part:32 * part + HEADS, 0, 0:KINDS * P], b_win).then_inc(b_in, 16)
            sp.dma_start(ub[:, 1, 0:T * P], heads_d).then_inc(b_in, 16)

            for t in range(T):
                sp.dma_start(xs[:, 0, t, :], x[0, t * P:(t + 1) * P, :]).then_inc(x_in[t], 16)
            sp.dma_start(wwin[:, :, :, :], w_win[:, 0:CORNERS]).then_inc(wwin_in, 16)
            sp.dma_start(wcor[:, :, :], w_win[0:2 * HD, CORNERS, :, 0:2 * HD]).then_inc(wwin_in, 16)
            for t in range(T):
                sp.wait_ge(x_in[t], 16)
                sp.dma_start(xs[:, 1, t, :], x[1, t * P:(t + 1) * P, :]).then_inc(x_in[t], 16)

            def load_next(n, par, t):
                sp.wait_ge(out_done[t], n * 16)
                sp.dma_start(xs[:, 1 - par, t, :], x[n + 1, t * P:(t + 1) * P, :]).then_inc(x_in[t], 16)

            def step(n, par, load):
                for t in range(T):
                    sp.wait_ge(added, (n - 1) * BACK + UNITS * (t + 1))
                    sp.dma_start(out[n - 1, t * P:(t + 1) * P, :], xs[:, 1 - par, t, :]).then_inc(out_done[t], 16)
                    if load and t > 0:
                        load_next(n, par, t - 1)
                if load:
                    load_next(n, par, T - 1)

            step(1, 1, True)
            with sp.Fori(0, (B - 4) // 2) as it:
                step(it * 2 + 2, 0, True)
                step(it * 2 + 3, 1, True)
            step(B - 2, 0, True)
            step(B - 1, 1, False)
            step(B, 0, False)
            for t in range(T):
                sp.wait_ge(out_done[t], B * 16)

        @block.gpsimd
        def _(pool):
            pool.memset(ub[:, :, :], 0.0)
            pool.memset(xp[:, :, :, :], 0.0)
            pool.memset(eps_s[:, :], EPS)
            pool.memset(mhalf[:, :], -0.5)
            pool.memset(ones_h[:, :], 1.0 / (P * H))
            pool.memset(ones_l[:, :], 1.0).then_inc(zeros_set, 1)

            def rsqrt(dst, src, k):
                return nc.gpsimd.tensor_tensor(dst, src, mhalf[:, 0:k], ALU.pow)

            def back_part(n, par):
                for t in range(T):
                    c = slice(t, t + 1)
                    pool.wait_ge(ve2_done, (n - 1) * T + t + 1)
                    rsqrt(r2[:, c], ve2[:, c], 1).then_inc(r2_done, 1)
                    pool.wait_ge(r2_done, (n - 1) * T + t + 1)
                    nc.gpsimd.tensor_tensor(nmr2[:, c], nm2[:, c], r2[:, c], ALU.mult).then_inc(nmr2_done, 1)
                    pool.wait_ge(nmr2_done, (n - 1) * T + t + 1)
                    pool.sem_inc(passed_pool, 1)
                    blocks = ub[:, t, :]
                    forms = ([blocks[:, 0:COLS * NB3].rearrange("p (k h c) -> p k h c", k=COLS, c=WS)]
                             + sides_in(blocks[:, COLS * NB3:]) + ends_in(blocks[:, (COLS + 1) * NB3:]))
                    for src, dst in zip(image_pieces(xs[:, 1 - par, t, :]), forms):
                        nc.gpsimd.tensor_scalar(dst, src, r2[:, c], nmr2[:, c], ALU.mult, ALU.add).then_inc(xn_done, 1)

            def step(pool, n, par, front, back):
                if back:
                    back_part(n, par)
                if not front:
                    return
                pool.wait_ge(ve1_done, n + 1)
                rsqrt(r1[:, :], ve1[:, :], T).then_inc(r1_done, 1)
                pool.wait_ge(vh_done, n + 1)
                rsqrt(rh[:, :], hv[:, 2, :], 8).then_inc(rh_done, 1)
                for t in range(T):
                    if t == T - 1:
                        pool.wait_ge(yvar_done, n + 1)
                        rsqrt(ry[:, :], yv[:, 1:2], 1).then_inc(ry_done, 1)
                    pool.wait_ge(wmax_done, n * T + t + 1)
                    m = image(ub[:, t, :])
                    g = th[:, 0, t, :].unsqueeze(2).broadcast_to([P, H, W])
                    nc.gpsimd.tensor_tensor(m, m, g, ALU.mult).then_inc(v_done, 1)

            step(pool, 0, 0, True, False)
            step(pool, 1, 1, True, True)
            with pool.Fori(0, (B - 2) // 2) as it:
                step(pool, it * 2 + 2, 0, True, True)
                step(pool, it * 2 + 3, 1, True, True)
            step(pool, B, 0, False, True)

        @block.scalar
        def _(act):
            def evac(n, t, units):
                for j in units:
                    k = UNITS * t + j
                    s = k % XT_SLOTS
                    wait(act, mix_ready, freed(n, k, XT_SLOTS))
                    act.wait_ge(xt_ready, (n - 1) * BACK + k + 1)
                    w = NB3 if j < UNITS - 1 else 4 * P
                    nc.scalar.activation(xt[:, s, 0:w], p_xt[k % XP_BANKS][:, 0:w], ACT.Copy).then_inc(xt_copied, 1)

            def step(act, n, par, front, back):
                def nm(t):
                    act.wait_ge(m2_ready, (n - 1) * T + t + 1)
                    nc.scalar.activation(nm2[:, t:t + 1], p_m2[:, t:t + 1], ACT.Copy, scale=-1.0).then_inc(nm2_done, 1)
                    act.wait_ge(nm2_done, (n - 1) * T + t + 1)
                    nc.scalar.activation(junk, xs[:, 1 - par, t, :], ACT.Square, bias=nm2[:, t:t + 1],
                                         accum_out=sq2[:, t:t + 1]).then_inc(sq2_done, 1)

                def ve(t):
                    act.wait_ge(v2_ready, (n - 1) * T + t + 1)
                    nc.scalar.activation(ve2[:, t:t + 1], p_v2[:, t:t + 1], ACT.Identity, bias=eps_s[:, :])\
                        .then_inc(ve2_done, 1)

                def square(t):
                    act.wait_ge(x_in[t], (n + 1) * 16)
                    nc.scalar.activation(junk, xs[:, par, t, :], ACT.Square, bias=nm1[:, t:t + 1],
                                         accum_out=sq1[:, t:t + 1]).then_inc(sq1_done, 1)

                if back:
                    for t in range(T):
                        if t == 0:
                            act.wait_ge(sq1_done, n * T)
                        else:
                            act.wait_ge(sq2_done, (n - 1) * T + t)
                        nm(t)
                        if t > 0:
                            ve(t - 1)
                    ve(T - 1)
                if front:
                    act.wait_ge(m1_ready, n + 1)
                    nc.scalar.activation(nm1[:, :], p_m1, ACT.Copy, scale=-1.0).then_inc(nm1_done, 1)
                    act.wait_ge(nm1_done, n + 1)
                for t in range(T):
                    if front:
                        wait(act, sq1_done, n * T + t)
                        square(t)
                    if back:
                        evac(n, 0, range(2 * t, 2 * t + 2))
                if front:
                    act.wait_ge(v1_ready, n + 1)
                    nc.scalar.activation(ve1[:, :], p_v1, ACT.Identity, bias=eps_s[:, :]).then_inc(ve1_done, 1)
                if back:
                    evac(n, 1, range(UNITS))
                if front:
                    act.wait_ge(fm_ready, n + 1)
                    nc.scalar.activation(fm[:, :], p_fm, ACT.Copy).then_inc(fm_done, 1)
                if back:
                    evac(n, 2, range(UNITS))
                if front:
                    act.wait_ge(hb_done, HB * (n + 1))
                    for d in range(2):
                        for t in range(T):
                            k = d * T + t
                            nc.scalar.activation(th[:, d, t, :], ff[:, 0, d, t, :], ACT.Tanh,
                                                 scale=hv[:, 1, k:k + 1], bias=hv[:, 3, k:k + 1]).then_inc(th_done, 1)
                if back:
                    evac(n, 3, range(UNITS))
                if front:
                    act.wait_ge(ym_ready, n + 1)
                    nc.scalar.activation(ym[:, :], p_ym, ACT.Copy, scale=float(P * H) / (C * L)).then_inc(ym_done, 1)
                    act.wait_ge(ynt_ready, n + 1)
                    nc.scalar.activation(ynt, p_col[0][0:L, :], ACT.Copy).then_inc(ynt_done, 1)
                    act.wait_ge(att_done, ATT * n + 3)
                    nc.scalar.activation(ee[:, 0, :, :], at[:, :, :], ACT.Exp).then_inc(exp_done, 1)
                    act.wait_ge(att_done, ATT * n + 7)
                    nc.scalar.activation(tc[:, :], oo[:, :], ACT.Tanh, scale=0.5).then_inc(tc_done, 1)

            act.wait_ge(zeros_set, 1)
            act.wait_ge(psum_clear, 1)
            step(act, 0, 0, True, False)
            step(act, 1, 1, True, True)
            with act.Fori(0, (B - 2) // 2) as it:
                step(act, it * 2 + 2, 0, True, True)
                step(act, it * 2 + 3, 1, True, True)
            step(act, B, 0, False, True)

        @block.tensor
        def _(pe):
            pe.wait_ge(psum_clear, 1)
            pe.wait_ge(zeros_set, 1)
            pe.wait_ge(consts_in, 16 * 13)
            pe.wait_ge(consts_set, 1)

            def step(pe, n, par, front, back):
                def colsum(t):
                    pe.wait_ge(x_in[t], (n + 1) * 16)
                    if t >= 2:
                        pe.wait_ge(colsum_read, n * T + t - 1)
                    elif t == 0:
                        wait(pe, ynt_done, n)
                    else:
                        wait(pe, att_done, ATT * (n - 1) + 4)
                    v = xs[:, par, t, :].rearrange("p (g f) -> p g f", f=4 * W)
                    o = p_col[t % 2][:, 0:4 * W]
                    for g in range(H // 4):
                        mm = pe.matmul(o, ident[:, :], v[:, g, :], start=(g == 0), stop=(g == H // 4 - 1))
                    mm.then_inc(colsum_ready, 1)

                def mean(t):
                    pe.wait_ge(x1_done, (n - 1) * T + t + 1)
                    wait(pe, nm2_done, (n - 1) * T + t)
                    wait(pe, ve2_done, (n - 1) * T + t - 1 if t else (n - 1) * T)
                    pe.matmul(p_m2[:, t:t + 1], gmean[:, :], s2[:, t:t + 1], start=True, stop=True).then_inc(m2_ready, 1)

                def var(t):
                    pe.wait_ge(sq2_done, (n - 1) * T + t + 1)
                    pe.wait_ge(nm2_done, (n - 1) * T + min(t + 2, T))
                    wait(pe, ve2_done, (n - 1) * T + t)
                    pe.matmul(p_v2[:, t:t + 1], gmean[:, :], sq2[:, t:t + 1], start=True, stop=True)\
                      .then_inc(v2_ready, 1)

                if front:
                    colsum(0)
                    colsum(1)
                if back:
                    mean(0)
                    mean(1)
                    var(0)
                    mean(2)
                    var(1)
                    mean(3)
                    var(2)
                    var(3)
                if front:
                    colsum(2)
                    colsum(3)
                if front:
                    pe.wait_ge(chsum_done, n + 1)
                    pe.matmul(p_m1, gmean[:, :], chs[:, :], start=True, stop=True).then_inc(m1_ready, 1)

                def turn(k):
                    t, j = divmod(k, UNITS)
                    if j == 0:
                        pe.wait_ge(xn_done, (n - 1) * XN * T + XN * t + 1)
                    if j >= COLS:
                        pe.wait_ge(xn_done, (n - 1) * XN * T + XN * t + (2 if j == COLS else XN))
                    wait(pe, xt_copied, freed(n, k, XP_BANKS))
                    ps = p_xt[k % XP_BANKS]
                    for b in range(3):
                        mm = pe.transpose(ps[:, b * P:(b + 1) * P], ub[:, t, j * NB3 + b * P:j * NB3 + (b + 1) * P],
                                          ident[:, :])
                    if j == UNITS - 1:
                        mm = pe.transpose(ps[0:64, 3 * P:4 * P], ub[:, t, HW - 64:HW], ident[:, :])
                    mm.then_inc(xt_ready, 1)

                def mix(k):
                    t, j = divmod(k, UNITS)
                    kind = kind_of(j)
                    s = k % XT_SLOTS
                    ps = p_y[k % Y_BANKS]
                    wait(pe, added, freed(n, k, Y_BANKS))
                    rhs = bpat[:, kind, :].unsqueeze(1).broadcast_to([P, 3, P])
                    pe.matmul(ps[:, 0:NB3], heads[:, t, :], rhs, start=True, stop=False, skip_group_check=True)
                    if j == UNITS - 1:
                        pe.matmul(ps[:, NB3:NB3 + 64], heads[:, t, :], bpat[:, CORNERS, 0:64], start=False, stop=False,
                                  skip_group_check=True)
                    pe.wait_ge(xt_copied, (n - 1) * BACK + k + 1)
                    nb = 4 if j == UNITS - 1 else 3
                    for b in range(nb):
                        for q in range(HPT):
                            rows = slice(HD * q, HD * (q + 1))
                            cols = slice(b * P + HD * q, b * P + HD * (q + 1))
                            if b == 3:
                                o, xb, wb = ps[rows, NB3:NB3 + 64], xt[0:64, s, cols], wcor[:, t * HPT + q, :]
                            else:
                                o, xb, wb = ps[rows, b * P:(b + 1) * P], xt[:, s, cols], wwin[:, kind, t * HPT + q, :]
                            mm = pe.matmul(o, xb, wb,
                                           start=False, stop=(b == nb - 1), skip_group_check=True,
                                           tile_position=(0, HD * q))
                    mm.then_inc(mix_ready, 1)

                for t in range(T):
                    if back:
                        for j in range(UNITS):
                            k = t * UNITS + j
                            if k == 0:
                                turn(0)
                            if k + 1 < BACK:
                                turn(k + 1)
                            mix(k)
                    if front and t == 0:
                        pe.wait_ge(sq1_done, (n + 1) * T)
                        pe.matmul(p_v1, gmean[:, :], sq1[:, :], start=True, stop=True).then_inc(v1_ready, 1)
                    if front and t == 1:
                        pe.wait_ge(fstat_done, n + 1)
                        pe.matmul(p_fm, ones_h[:, :], fs[:, :], start=True, stop=True).then_inc(fm_ready, 1)
                if not front:
                    return
                pe.wait_ge(ystat_done, n + 1)
                pe.matmul(p_ym, ones_h[:, :], ys[:, :], start=True, stop=True).then_inc(ym_ready, 1)
                pe.wait_ge(yn_done, T * (n + 1))
                pe.wait_ge(colsum_read, T * (n + 1))
                pe.sem_inc(passed_pe, 1)
                for t in range(T):
                    mm = pe.transpose(p_col[0][0:L, t * P:(t + 1) * P], y[:, t, :], ident[:, :])
                mm.then_inc(ynt_ready, 1)
                pe.wait_ge(ynt_done, n + 1)
                pe.sem_inc(passed_pe, 1)
                for t in range(T):
                    for q in range(HPT):
                        rows = slice(HD * q, HD * (q + 1))
                        cols = slice(t * P + HD * q, t * P + HD * (q + 1))
                        pe.matmul(p_gram[rows, HD * t:HD * (t + 1)], ynt[:, cols], ynt[:, cols],
                                  start=True, stop=True, tile_position=(0, HD * q))
                for q in range(HPT):
                    rows = slice(HD * q, HD * (q + 1))
                    v = ynt.rearrange("p (t q c) -> p t q c", t=T, q=HPT)[:, :, q, :]
                    mm = pe.matmul(p_vb[rows, :], ones_l[:, :], v, start=True, stop=True, tile_position=(0, HD * q))
                mm.then_inc(gram_ready, 1)

            step(pe, 0, 0, True, False)
            pe.wait_ge(wwin_in, 32)
            step(pe, 1, 1, True, True)
            with pe.Fori(0, (B - 2) // 2) as it:
                step(pe, it * 2 + 2, 0, True, True)
                step(pe, it * 2 + 3, 1, True, True)
            step(pe, B, 0, False, True)

        @block.vector
        def _(dve):
            v = nc.vector
            for ps in p_xt + p_y + p_col + [p_front, p_back]:
                last = v.memset(ps[:, :], 0.0)
            last.then_inc(psum_clear, 1)
            dve.wait_ge(zeros_set, 1)
            dve.wait_ge(b_in, 16 * 4)
            v.memset(bpat[:, :, :], 0.0).then_inc(split, 1)
            v.tensor_copy(heads[:, :, :].rearrange("p t c -> p (t c)"), ub[:, 1, 0:T * P])
            bsrc = ub[:, 0, 0:KINDS * P]
            part = junk[:, 0:KINDS * P]
            dve.wait_ge(split, 1)
            done = 1
            for k in range(3):
                v.tensor_copy(part, bsrc).then_inc(split, 1)
                done += 1
                dve.wait_ge(split, done)
                v.tensor_copy(bpat[32 * k:32 * (k + 1), :, :].rearrange("p k c -> p (k c)"),
                              part[32 * k:32 * (k + 1), :])
                v.tensor_tensor(bsrc, bsrc, part, ALU.subtract).then_inc(split, 1)
                done += 1
                dve.wait_ge(split, done)
            dve.wait_ge(consts_in, 16 * 13)
            for t in range(T):
                v.tensor_scalar(wqk_s[:, t, :], wqk_s[:, t, :], gmb[:, 6, t:t + 1], float(HD) ** -0.5, ALU.mult, ALU.mult)
            v.tensor_scalar(wv_s[:, :, :], wv_s[:, :, :], 1.0 / L, None, ALU.mult)
            v.tensor_scalar(gmb[:, 0:4, :], gmb[:, 0:4, :], 0.5, None, ALU.mult).then_inc(consts_set, 1)
            dve.wait_ge(consts_set, 1)

            def step(dve, n, par, front, back):
                def bcast(ap, w):
                    return ap.unsqueeze(2).broadcast_to([P, ap.shape[1], w])

                def add_units(t, units):
                    for j in units:
                        k = UNITS * t + j
                        ps = p_y[k % Y_BANKS]
                        dve.wait_ge(mix_ready, (n - 1) * BACK + k + 1)
                        if j < COLS:
                            m = image(xs[:, 1 - par, t, :])[:, SHIFT:SHIFT + IN, SHIFT + WS * j:SHIFT + WS * (j + 1)]
                            pairs = [(m, ps[:, 0:NB3].rearrange("p (h c) -> p h c", c=WS))]
                        else:
                            im = image_pieces(xs[:, 1 - par, t, :])
                            pairs = zip(im[1:2], sides_in(ps)) if j == COLS else zip(im[2:], ends_in(ps))
                        for m, product in pairs:
                            ins = v.tensor_tensor(m, product, m, ALU.add)
                        ins.then_inc(added, 1)

                def sums():
                    for t in range(T):
                        dve.wait_ge(x_in[t], (n + 1) * 16)
                        v.tensor_reduce(rs[:, 0, t, :], image(xs[:, par, t, :]), AX.X, ALU.add).then_inc(rowsum_done, 1)
                        dve.wait_ge(colsum_ready, n * T + t + 1)
                        v.tensor_reduce(rs[:, 1, t, :], p_col[t % 2][:, 0:4 * W].rearrange(
                            "p (f w) -> p w f", w=W), AX.X, ALU.add).then_inc(colsum_read, 1)
                    dve.wait_ge(rowsum_done, (n + 1) * T)
                    v.tensor_reduce(chs[:, :], rs[:, 0, :, :], AX.X, ALU.add).then_inc(chsum_done, 1)

                def convs():
                    dve.wait_ge(nm1_done, n + 1)
                    dve.wait_ge(colsum_read, (n + 1) * T)
                    for d in range(2):
                        v.scalar_tensor_tensor(xp[:, d, :, PAD:PAD + H], bcast(nm1[:, :], H), float(H), rs[:, d, :, :],
                                               ALU.mult, ALU.add).then_inc(centred, 1)
                    dve.wait_ge(centred, 2 * (n + 1))
                    count, last = 0, {}
                    for tap in range(max(KS)):
                        for d in range(2):
                            for t in range(T):
                                if tap >= KS[t]:
                                    continue
                                src = xp[:, d, t, PAD + tap - KS[t] // 2:PAD + tap - KS[t] // 2 + H]
                                wi = sum(KS[:t]) + tap
                                dst = ff[:, 0, d, t, :]
                                if tap == 0:
                                    ins = v.tensor_scalar(dst, src, wc[:, d, wi:wi + 1], None, ALU.mult)
                                else:
                                    dve.wait_ge(tap_done, TAPS2 * n + last[d, t])
                                    ins = v.scalar_tensor_tensor(dst, src, wc[:, d, wi:wi + 1], dst, ALU.mult, ALU.add)
                                ins.then_inc(tap_done, 1)
                                count += 1
                                last[d, t] = count
                    assert count == TAPS2

                def conv_stats():
                    dve.wait_ge(r1_done, n + 1)
                    dve.wait_ge(tap_done, TAPS2 * (n + 1))
                    for d in range(2):
                        v.scalar_tensor_tensor(ff[:, 0, d, :, :], ff[:, 0, d, :, :], 1.0 / H, bcast(r1[:, :], H),
                                               ALU.mult, ALU.mult).then_inc(f_done, 1)
                    dve.wait_ge(f_done, F3 * n + 2)
                    f = ff[:, 0, :, :, :].rearrange("p d t h -> p (d t) h")
                    v.tensor_tensor(f, f, bcast(bc[:, :, :].rearrange("p d t -> p (d t)"), H), ALU.add).then_inc(f_done, 1)
                    dve.wait_ge(f_done, F3 * n + 3)
                    v.tensor_tensor(ff[:, 1, :, :, :], ff[:, 0, :, :, :], ff[:, 0, :, :, :], ALU.mult).then_inc(f_done, 1)
                    dve.wait_ge(f_done, F3 * (n + 1))
                    v.tensor_reduce(fs[:, :], ff[:, :, :, :, :].rearrange("p a d t h -> p (a d t) h"), AX.X, ALU.add)\
                     .then_inc(fstat_done, 1)

                def gate_var():
                    dve.wait_ge(fm_done, n + 1)
                    v.tensor_tensor(hv[:, 0, :], fm[:, 0:8], fm[:, 0:8], ALU.mult).then_inc(gv, 1)
                    dve.wait_ge(gv, 2 * n + 1)
                    v.tensor_tensor(hv[:, 0, :], fm[:, 8:16], hv[:, 0, :], ALU.subtract).then_inc(gv, 1)
                    dve.wait_ge(gv, 2 * n + 2)
                    v.tensor_scalar(hv[:, 2, :], hv[:, 0, :], 0.0, EPS, ALU.max, ALU.add).then_inc(vh_done, 1)

                def gate_affine():
                    dve.wait_ge(rh_done, n + 1)
                    v.tensor_tensor(hv[:, 1, :], rh[:, :], gmb[:, 0:2, :].rearrange("p a t -> p (a t)"), ALU.mult)\
                     .then_inc(hb_done, 1)
                    dve.wait_ge(hb_done, HB * n + 1)
                    v.tensor_tensor(hv[:, 3, :], fm[:, 0:8], hv[:, 1, :], ALU.mult).then_inc(hb_done, 1)
                    dve.wait_ge(hb_done, HB * n + 2)
                    v.tensor_tensor(hv[:, 3, :], gmb[:, 2:4, :].rearrange("p a t -> p (a t)"), hv[:, 3, :],
                                    ALU.subtract).then_inc(hb_done, 1)

                def gates():
                    dve.wait_ge(th_done, 2 * T * (n + 1))
                    v.scalar_tensor_tensor(th[:, 0, :, :], th[:, 0, :, :], 1.0, bcast(r1[:, :], H), ALU.add, ALU.mult)\
                     .then_inc(gate_done, 1)
                    v.tensor_scalar(th[:, 1, :, :], th[:, 1, :, :], 0.25, 0.25, ALU.mult, ALU.add).then_inc(gate_done, 1)

                def gated(t):
                    if t == 0:
                        dve.wait_ge(gate_done, 2 * (n + 1))
                    if not (isinstance(n, int) and n == 0):
                        dve.wait_ge(xt_ready, (n - 1) * BACK + UNITS * (t + 1))
                    m = image(ub[:, t, :])
                    g = th[:, 1, t, :].unsqueeze(1).broadcast_to([P, H, W])
                    v.scalar_tensor_tensor(m, image(xs[:, par, t, :]), nm1[:, t:t + 1], g, ALU.add, ALU.mult)\
                     .then_inc(u_done, 1)
                    dve.wait_ge(u_done, n * T + t + 1)
                    q = pm[:, :]
                    wait(dve, y_done, n * T + t)
                    v.tensor_reduce(q, ub[:, t, :].rearrange("p (k w) -> p k w", w=WIN), AX.X, ALU.max)\
                     .then_inc(wmax_done, 1)
                    dve.wait_ge(wmax_done, n * T + t + 1)
                    q3 = q.rearrange("p (h k) -> p h k", k=NW)
                    v.tensor_tensor(q3, q3, bcast(th[:, 0, t, :], NW), ALU.mult).then_inc(wgate_done, 1)
                    dve.wait_ge(wgate_done, n * T + t + 1)
                    v.tensor_reduce(y[:, t, :], q.rearrange("p (a r k) -> p a k r", r=WIN, k=NW), AX.X, ALU.max)\
                     .then_inc(y_done, 1)

                def pooled_norm():
                    dve.wait_ge(y_done, T * (n + 1))
                    yf = y[:, :, :].rearrange("p t l -> p (t l)")
                    v.tensor_reduce(ys[:, 0:1], yf, AX.X, ALU.add)
                    v.scalar_tensor_tensor(yj, yf, 1.0, yf, ALU.mult, ALU.mult, accum_out=ys[:, 1:2])\
                     .then_inc(ystat_done, 1)
                    dve.wait_ge(ym_done, n + 1)
                    v.tensor_tensor(yv[:, 0:1], ym[:, 0:1], ym[:, 0:1], ALU.mult).then_inc(yq, 1)
                    dve.wait_ge(yq, 5 * n + 1)
                    v.tensor_tensor(yv[:, 0:1], ym[:, 1:2], yv[:, 0:1], ALU.subtract).then_inc(yq, 1)
                    dve.wait_ge(yq, 5 * n + 2)
                    v.tensor_scalar(yv[:, 1:2], yv[:, 0:1], 0.0, EPS, ALU.max, ALU.add).then_inc(yvar_done, 1)
                    dve.wait_ge(ry_done, n + 1)
                    v.tensor_scalar(ab[:, 0, :], gmb[:, 4, :], ry[:, 0:1], None, ALU.mult).then_inc(yq, 1)
                    dve.wait_ge(yq, 5 * n + 3)
                    v.tensor_scalar(ab[:, 1, :], ab[:, 0, :], ym[:, 0:1], None, ALU.mult).then_inc(yq, 1)
                    dve.wait_ge(yq, 5 * n + 4)
                    v.tensor_tensor(ab[:, 2, :], gmb[:, 5, :], ab[:, 1, :], ALU.subtract).then_inc(yq, 1)
                    dve.wait_ge(yq, 5 * n + 5)
                    for t in range(T):
                        v.tensor_scalar(y[:, t, :], y[:, t, :], ab[:, 0, t:t + 1], ab[:, 2, t:t + 1],
                                        ALU.mult, ALU.add).then_inc(yn_done, 1)

                def attention():
                    g = p_gram.rearrange("p (t c) -> p t c", t=T)
                    vb = p_vb.rearrange("p (t c) -> p t c", t=T)
                    dve.wait_ge(gram_ready, n + 1)
                    v.tensor_tensor(at[:, :, :], g, wqk_s[:, :, :], ALU.mult).then_inc(att_done, 1)
                    dve.wait_ge(att_done, ATT * n + 1)
                    v.tensor_reduce(mx[:, :], at[:, :, :], AX.X, ALU.max).then_inc(att_done, 1)
                    dve.wait_ge(att_done, ATT * n + 2)
                    v.tensor_tensor(at[:, :, :], at[:, :, :], bcast(mx[:, :], HD), ALU.subtract).then_inc(att_done, 1)
                    v.tensor_tensor(ee[:, 1, :, :], vb, wv_s[:, :, :], ALU.mult).then_inc(att_done, 1)
                    dve.wait_ge(exp_done, n + 1)
                    dve.wait_ge(att_done, ATT * n + 4)
                    v.tensor_tensor(ee[:, 1, :, :], ee[:, 0, :, :], ee[:, 1, :, :], ALU.mult).then_inc(att_done, 1)
                    dve.wait_ge(att_done, ATT * n + 5)
                    v.tensor_reduce(ss[:, :, :].rearrange("p a t -> p (a t)"),
                                    ee[:, :, :, :].rearrange("p a t c -> p (a t) c"), AX.X, ALU.add).then_inc(att_done, 1)
                    dve.wait_ge(att_done, ATT * n + 6)
                    v.reciprocal(rd[:, :], ss[:, 0, :]).then_inc(rdone, 1)
                    dve.wait_ge(rdone, n + 1)
                    v.tensor_tensor(oo[:, :], ss[:, 1, :], rd[:, :], ALU.mult).then_inc(att_done, 1)
                    dve.wait_ge(tc_done, n + 1)
                    v.tensor_scalar(ca[:, :], tc[:, :], 0.5, 0.5, ALU.mult, ALU.add).then_inc(ca_done, 1)
                    dve.wait_ge(ca_done, n + 1)

                def first_out():
                    for t in range(T):
                        dve.wait_ge(v_done, n * T + t + 1)
                        v.scalar_tensor_tensor(xs[:, par, t, :], ub[:, t, :], ca[:, t:t + 1], xs[:, par, t, :],
                                               ALU.mult, ALU.add, accum_out=s2[:, t:t + 1]).then_inc(x1_done, 1)

                if front:
                    sums()
                    convs()
                if back:
                    add_units(0, range(UNITS))
                if front:
                    conv_stats()
                if back:
                    add_units(1, range(UNITS))
                if front:
                    gate_var()
                if back:
                    add_units(2, range(0, 4))
                if front:
                    gate_affine()
                if back:
                    add_units(2, range(4, UNITS))
                if front:
                    gates()
                    gated(0)
                    gated(1)
                if back:
                    add_units(3, range(UNITS))
                if front:
                    gated(2)
                    gated(3)
                    pooled_norm()
                    attention()
                    first_out()

            step(dve, 0, 0, True, False)
            step(dve, 1, 1, True, True)
            with dve.Fori(0, (B - 2) // 2) as it:
                step(dve, it * 2 + 2, 0, True, True)
                step(dve, it * 2 + 3, 1, True, True)
            step(dve, B, 0, False, True)


def window_weights(w):
    out = np.zeros((P, KINDS, HEADS, P), w.dtype)
    for kind in range(KINDS):
        places = block_positions(kind)
        for win in range(4):
            at = [p for p, (v, _) in enumerate(places) if v == win]
            if at:
                pos = [places[p][1] for p in at]
                out[np.array(at)[:, None], kind, :, np.array(at)[None, :]] = w[:, pos][:, :, pos].transpose(2, 1, 0)
    return out


def window_bias(b):
    out = np.zeros((HEADS, KINDS, P), b.dtype)
    for kind in range(KINDS):
        places = block_positions(kind)
        out[:, kind, :len(places)] = b[:, [pos for _, pos in places]]
    return out.reshape(HEADS, KINDS * P)


def shape_constants():
    ident = np.eye(P, dtype=np.float32)
    gmean = np.kron(np.eye(P // GROUP), np.full((GROUP, GROUP), 1.0 / (GROUP * HW))).astype(np.float32)
    heads = np.zeros((P, T, P), np.float32)
    for part in range(3):
        for head in range(HEADS):
            t, q = divmod(head, HPT)
            heads[32 * part + head, t, HD * q:HD * (q + 1)] = 1.0
    return ident, gmean, heads.reshape(P, T * P)


def kernel(**inputs):
    import concourse.bacc as bacc
    from concourse.bass_utils import run_bass_kernel_spmd as run

    a = {k: np.asarray(v) for k, v in inputs.items()}
    g = {k[len("L0_conv_"):]: v for k, v in a.items() if k.startswith("L0_conv_")}

    def per_tile(names):
        return np.concatenate([g[k].reshape(P, -1) for k in names], axis=1)

    hs, ws = ("lh", "sh", "mh", "gh"), ("lw", "sw", "mw", "gw")
    ident, gmean, heads = shape_constants()
    arrays = {
        "x": np.ascontiguousarray(a["x"]).reshape(B, C, HW),
        "w_conv": np.ascontiguousarray(np.stack([per_tile(["w_" + k for k in hs]), per_tile(["w_" + k for k in ws])], 1)),
        "b_conv": np.ascontiguousarray(np.stack([per_tile(["b_" + k for k in hs]), per_tile(["b_" + k for k in ws])], 1)),
        "gam": np.ascontiguousarray(np.stack([g[k].reshape(T, P).T for k in (
            "gn_h_g", "gn_w_g", "gn_h_b", "gn_w_b", "gn_g", "gn_b", "wq")], 1)),
        "wk": np.ascontiguousarray(g["wk"]),
        "wv": np.ascontiguousarray(g["wv"]),
        "w_win": window_weights(a["L1_conv_w"]),
        "b_win": window_bias(a["L1_conv_b"]),
        "ident": ident,
        "gmean": gmean,
        "heads": heads,
    }
    nc = bacc.Bacc("TRN2", target_bir_lowering=False, num_devices=1)
    args = [nc.dram_tensor(k + "_in", v.shape, mybir.dt.from_np(v.dtype), kind="ExternalInput").ap() for k, v in arrays.items()]
    out = nc.dram_tensor("out", (B, C, HW), F32, kind="ExternalOutput").ap()
    build(nc, *args, out)
    got = run(nc, [{k + "_in": v for k, v in arrays.items()}], core_ids=[0]).results[0]["out"]
    return got.reshape(B, C, H, W)
```

```python
import numpy as np
from contextlib import ExitStack

import concourse.bass as bass
from concourse import mybir

F32 = mybir.dt.float32
BF16 = mybir.dt.bfloat16
ALU = mybir.AluOpType
ACT = mybir.ActivationFunctionType
AX = mybir.AxisListType

B, C, H, W = 32, 512, 56, 56
P = 128
T = C // P
HW = H * W
KS = (3, 5, 7, 9)
NTAPS = sum(KS)
PADW = 64
PAD = 4
WIN = 7
NW = H // WIN
L = NW * NW
HEADS, HD = 16, 32
HPT = P // HD
WS, SHIFT = 8, 4
KINDS = 4
INTERIOR, SIDES, ENDS, CORNERS = range(KINDS)
COLS = 6
UNITS = COLS + 2
IN = H - 2 * SHIFT
NB3 = 3 * P
XT_SLOTS = 3
XP_BANKS = 2
Y_BANKS = 4
FOLDED = 2
GROUP = 16
EPS = 1e-5


def block_positions(kind):
    out = []
    for w in range(2 if kind != CORNERS else 1):
        if kind == INTERIOR:
            out += [(w, r * WS + c) for r in range(WS) for c in range(WS)]
        elif kind == SIDES:
            out += [(2 * w + side, r * WS + SHIFT * (1 - side) + c)
                    for r in range(WS) for side in range(2) for c in range(SHIFT)]
        elif kind == ENDS:
            out += [(2 * w + end, (SHIFT * (1 - end) + r) * WS + c)
                    for end in range(2) for r in range(SHIFT) for c in range(WS)]
        else:
            out += [(2 * end + side, (SHIFT * (1 - end) + r) * WS + SHIFT * (1 - side) + c)
                    for end in range(2) for r in range(SHIFT) for side in range(2) for c in range(SHIFT)]
    return out


def build(nc, x, w_conv, b_conv, gam, wk, wv, w_win, b_win, ident_d, gmean_d, heads_d, out):
    with ExitStack() as ctx:
        def sb(name, shape, dt=F32):
            return ctx.enter_context(nc.sbuf_tensor(name, shape, dt))

        def pb(name):
            return ctx.enter_context(nc.psum_tensor(name, [P, 512], F32))

        def sem(name):
            return ctx.enter_context(nc.semaphore(name))

        ident = sb("ident", [P, P])
        gmean = sb("gmean", [P, P])
        ones_h = sb("ones_h", [P, P])
        ones_l = sb("ones_l", [L, HD])
        heads = sb("heads", [P, T, P], BF16)
        bpat = sb("bpat", [P, KINDS, P], BF16)
        wwin = sb("wwin", [P, KINDS - 1, HEADS, P])
        wcor = sb("wcor", [2 * HD, HEADS, 2 * HD])
        wc = sb("wc", [P, 2, NTAPS])
        bc = sb("bc", [P, 2, T])
        gmb = sb("gmb", [P, 7, T])
        wqk_s = sb("wqk_s", [P, T, HD])
        wv_s = sb("wv_s", [P, T, HD])
        eps_s = sb("eps_s", [P, 1])
        mhalf = sb("mhalf", [P, 8])
        xs = sb("xs", [P, 2, T, HW])
        ub = sb("ub", [P, T, HW])
        spare = sb("spare", [P, HW // 2])
        junk = spare[:, :].bitcast(BF16)
        fold = spare[:, :].rearrange("p (h w) -> p h w", w=W // 2)
        xt = sb("xt", [P, XT_SLOTS, 4 * P])
        ynt = xt[0:L, 0, :]
        yj = xt[:, 1, 0:T * L]
        rs = sb("rs", [P, 2, T, H])
        chs = sb("chs", [P, T])
        nm1 = sb("nm1", [P, T])
        sq1 = sb("sq1", [P, T])
        ve1 = sb("ve1", [P, T])
        r1 = sb("r1", [P, T])
        xp = sb("xp", [P, 2, T, PADW])
        ff = sb("ff", [P, 2, 2, T, H])
        fs = sb("fs", [P, 16])
        fm = sb("fm", [P, 16])
        hv = sb("hv", [P, 4, 8])
        rh = sb("rh", [P, 8])
        th = sb("th", [P, 2, T, H])
        pm = sb("pm", [P, H * NW])
        y = sb("y", [P, T, L])
        ys = sb("ys", [P, 2])
        ym = sb("ym", [P, 2])
        yv = sb("yv", [P, 2])
        ry = sb("ry", [P, 1])
        ab = sb("ab", [P, 3, T])
        at = sb("at", [P, T, HD])
        mx = sb("mx", [P, T])
        ee = sb("ee", [P, 2, T, HD])
        ss = sb("ss", [P, 2, T])
        rd = sb("rd", [P, T])
        oo = sb("oo", [P, T])
        tc = sb("tc", [P, T])
        ca = sb("ca", [P, T])
        s2 = sb("s2", [P, T])
        nm2 = sb("nm2", [P, T])
        sq2 = sb("sq2", [P, T])
        ve2 = sb("ve2", [P, T])
        r2 = sb("r2", [P, T])
        nmr2 = sb("nmr2", [P, T])

        p_xt = [pb(f"p_xt{i}") for i in range(XP_BANKS)]
        p_y = [pb(f"p_y{i}") for i in range(Y_BANKS)]
        p_col = p_y
        p_front, p_back = pb("p_front"), pb("p_back")
        p_ynt = p_xt[0][0:L, :]
        p_gram, p_vb = p_xt[1][:, 0:P], p_xt[1][:, P:2 * P]
        p_m1, p_v1, p_fm, p_ym = p_front[:, 0:T], p_front[:, 8:12], p_front[:, 16:32], p_front[:, 32:34]
        p_m2, p_v2 = p_back[:, 0:4], p_back[:, 8:12]

        consts_in, wwin_in, b_in = sem("consts_in"), sem("wwin_in"), sem("b_in")
        psum_clear, zeros_set, consts_set = sem("psum_clear"), sem("zeros_set"), sem("consts_set")
        split = sem("split")
        x_in = [sem(f"x_in{t}") for t in range(T)]
        out_done = [sem(f"out_done{t}") for t in range(T)]
        rowsum_done, colsum_ready, colsum_read, chsum_done = (
            sem("rowsum_done"), sem("colsum_ready"), sem("colsum_read"), sem("chsum_done"))
        m1_ready, nm1_done, sq1_done, v1_ready, ve1_done, r1_done = (
            sem("m1_ready"), sem("nm1_done"), sem("sq1_done"), sem("v1_ready"), sem("ve1_done"), sem("r1_done"))
        centred, tap_done, f_done, fstat_done = sem("centred"), sem("tap_done"), sem("f_done"), sem("fstat_done")
        fm_ready, fm_done, vh_done, rh_done, hb_done, th_done, gate_done = (
            sem("fm_ready"), sem("fm_done"), sem("vh_done"), sem("rh_done"), sem("hb_done"), sem("th_done"),
            sem("gate_done"))
        u_done, fold_done, wmax_done, wgate_done, y_done, v_done = (
            sem("u_done"), sem("fold_done"), sem("wmax_done"), sem("wgate_done"), sem("y_done"), sem("v_done"))
        ystat_done, ym_ready, ym_done, yvar_done, ry_done, yn_done = (
            sem("ystat_done"), sem("ym_ready"), sem("ym_done"), sem("yvar_done"), sem("ry_done"), sem("yn_done"))
        ynt_ready, ynt_done, gram_ready, att_done, exp_done, tc_done, ca_done, x1_done, scaled_done, last_x1_done, last_sum_done = (
            sem("ynt_ready"), sem("ynt_done"), sem("gram_ready"), sem("att_done"), sem("exp_done"), sem("tc_done"),
            sem("ca_done"), sem("x1_done"), sem("scaled_done"), sem("last_x1_done"), sem("last_sum_done"))
        m2_ready, nm2_done, sq2_done, v2_ready, ve2_done, r2_done, nmr2_done, xn_done = (
            sem("m2_ready"), sem("nm2_done"), sem("sq2_done"), sem("v2_ready"), sem("ve2_done"), sem("r2_done"),
            sem("nmr2_done"), sem("xn_done"))
        passed_pool, passed_pe = sem("passed_pool"), sem("passed_pe")
        gv, yq, rdone = sem("gate_var_step"), sem("pooled_norm_step"), sem("recip_done")
        xt_ready, xt_copied, mix_ready, added = sem("xt_ready"), sem("xt_copied"), sem("mix_ready"), sem("added")

        block = ctx.enter_context(nc.Block())

        TAPS2 = 2 * NTAPS
        ATT = 7
        XN = 6
        F3 = 4
        HB = 3
        BACK = UNITS * T

        def freed(n, k, places):
            return (n - 1) * BACK + (k - places + 1 if k >= places else 0)

        def wait(eng, s, value):
            if not (isinstance(value, int) and value <= 0):
                eng.wait_ge(s, value)

        def image(ap):
            return ap.rearrange("p (h w) -> p h w", w=W)

        def kind_of(j):
            return INTERIOR if j < COLS else (SIDES if j == COLS else ENDS)

        def image_pieces(t_map):
            m = image(t_map)
            ends = m.rearrange("p (e r) w -> p e r w", r=SHIFT)
            mid = m[:, SHIFT:SHIFT + IN, :]
            return ([mid[:, :, SHIFT:SHIFT + IN].rearrange("p h (k c) -> p k h c", c=WS),
                     mid.rearrange("p h (s c) -> p h s c", c=SHIFT)[:, :, 0:14:13, :]]
                    + [ends[:, 13 * e, :, SHIFT:SHIFT + IN].rearrange("p r (k c) -> p k r c", c=WS) for e in range(2)]
                    + [ends[:, 13 * e].rearrange("p r (s c) -> p r s c", c=SHIFT)[:, :, 0:14:13, :] for e in range(2)])

        def sides_in(unit):
            return [unit[:, 0:NB3].rearrange("p (h s c) -> p h s c", s=2, c=SHIFT)]

        def ends_in(unit):
            e4 = unit[:, 0:NB3].rearrange("p (k e r c) -> p e k r c", e=2, r=SHIFT, c=WS)
            c4 = unit[:, NB3:NB3 + 64].rearrange("p (e r s c) -> p e r s c", e=2, r=SHIFT, s=2)
            return [e4[:, 0], e4[:, 1], c4[:, 0], c4[:, 1]]

        @block.sync
        def _(sp):
            for dst, src in ((ident[:, :], ident_d), (gmean[:, :], gmean_d), (wc[:, :, :], w_conv), (bc[:, :, :], b_conv),
                             (gmb[:, :, :], gam)):
                sp.dma_start(dst, src).then_inc(consts_in, 16)
            for q in range(HPT):
                rows = slice(HD * q, HD * (q + 1))
                wk_v = wk.rearrange("(t q c) -> q t c", q=HPT, c=HD)[q:q + 1].broadcast_to([HD, T, HD])
                wv_v = wv.rearrange("(t q c) -> q t c", q=HPT, c=HD)[q:q + 1].broadcast_to([HD, T, HD])
                sp.dma_start(wqk_s[rows, :, :], wk_v).then_inc(consts_in, 16)
                sp.dma_start(wv_s[rows, :, :], wv_v).then_inc(consts_in, 16)
            sp.wait_ge(zeros_set, 1)
            for part in range(3):
                sp.dma_start(ub[32 * part:32 * part + HEADS, 0, 0:KINDS * P], b_win).then_inc(b_in, 16)
            sp.dma_start(ub[:, 1, 0:T * P], heads_d).then_inc(b_in, 16)

            for t in range(T):
                sp.dma_start(xs[:, 0, t, :], x[0, t * P:(t + 1) * P, :]).then_inc(x_in[t], 16)
            sp.dma_start(wwin[:, :, :, :], w_win[:, 0:CORNERS]).then_inc(wwin_in, 16)
            sp.dma_start(wcor[:, :, :], w_win[0:2 * HD, CORNERS, :, 0:2 * HD]).then_inc(wwin_in, 16)
            for t in range(T):
                sp.wait_ge(x_in[t], 16)
                sp.dma_start(xs[:, 1, t, :], x[1, t * P:(t + 1) * P, :]).then_inc(x_in[t], 16)

            def load_next(n, par, t):
                sp.wait_ge(out_done[t], n * 16)
                sp.dma_start(xs[:, 1 - par, t, :], x[n + 1, t * P:(t + 1) * P, :]).then_inc(x_in[t], 16)

            def step(n, par, load):
                for t in range(T):
                    sp.wait_ge(added, (n - 1) * BACK + UNITS * (t + 1))
                    sp.dma_start(out[n - 1, t * P:(t + 1) * P, :], xs[:, 1 - par, t, :]).then_inc(out_done[t], 16)
                    if load:
                        load_next(n, par, t)

            step(1, 1, True)
            with sp.Fori(0, (B - 4) // 2) as it:
                step(it * 2 + 2, 0, True)
                step(it * 2 + 3, 1, True)
            step(B - 2, 0, True)
            step(B - 1, 1, False)
            step(B, 0, False)
            for t in range(T):
                sp.wait_ge(out_done[t], B * 16)

        @block.gpsimd
        def _(pool):
            pool.memset(ub[:, :, :], 0.0)
            pool.memset(xp[:, :, :, :], 0.0)
            pool.memset(eps_s[:, :], EPS)
            pool.memset(mhalf[:, :], -0.5)
            pool.memset(ones_h[:, :], 1.0 / (P * H))
            pool.memset(ones_l[:, :], 1.0).then_inc(zeros_set, 1)

            def rsqrt(dst, src, k):
                return nc.gpsimd.tensor_tensor(dst, src, mhalf[:, 0:k], ALU.pow)

            def normalise(n, par, t):
                c = slice(t, t + 1)
                pool.wait_ge(ve2_done, (n - 1) * T + t + 1)
                rsqrt(r2[:, c], ve2[:, c], 1).then_inc(r2_done, 1)
                pool.wait_ge(r2_done, (n - 1) * T + t + 1)
                nc.gpsimd.tensor_tensor(nmr2[:, c], nm2[:, c], r2[:, c], ALU.mult).then_inc(nmr2_done, 1)
                pool.wait_ge(nmr2_done, (n - 1) * T + t + 1)
                pool.sem_inc(passed_pool, 1)
                blocks = ub[:, t, :]
                forms = ([blocks[:, 0:COLS * NB3].rearrange("p (k h c) -> p k h c", k=COLS, c=WS)]
                         + sides_in(blocks[:, COLS * NB3:]) + ends_in(blocks[:, (COLS + 1) * NB3:]))
                for src, dst in zip(image_pieces(xs[:, 1 - par, t, :]), forms):
                    nc.gpsimd.tensor_scalar(dst, src, r2[:, c], nmr2[:, c], ALU.mult, ALU.add).then_inc(xn_done, 1)

            def step(n, par, front, back, ahead):
                if front:
                    pool.wait_ge(ve1_done, n + 1)
                    rsqrt(r1[:, :], ve1[:, :], T).then_inc(r1_done, 1)
                if back:
                    normalise(n, par, 0)
                    normalise(n, par, 1)
                    normalise(n, par, 2)
                if front:
                    pool.wait_ge(vh_done, n + 1)
                    rsqrt(rh[:, :], hv[:, 2, :], 8).then_inc(rh_done, 1)
                if back:
                    normalise(n, par, 3)
                if not front:
                    return
                def fold_columns(m, mpar, t):
                    pool.wait_ge(x_in[t], (m + 1) * 16)
                    if t == 0:
                        pool.wait_ge(sq1_done, m * T)
                        if back:
                            pool.wait_ge(sq2_done, n * T)
                    else:
                        pool.wait_ge(rowsum_done, m * T + t)
                    pool.sem_inc(passed_pool, 1)
                    f = image(xs[:, mpar, t, :])
                    nc.gpsimd.tensor_tensor(fold, f[:, :, 0:W // 2], f[:, :, W // 2:W], ALU.add).then_inc(fold_done, 1)

                for t in range(T):
                    if t == T - 1:
                        pool.wait_ge(yvar_done, n + 1)
                        rsqrt(ry[:, :], yv[:, 1:2], 1).then_inc(ry_done, 1)
                    pool.wait_ge(wmax_done, n * T + t + 1)
                    m = image(ub[:, t, :])
                    g = th[:, 0, t, :].unsqueeze(2).broadcast_to([P, H, W])
                    nc.gpsimd.tensor_tensor(m, m, g, ALU.mult).then_inc(v_done, 1)
                    if ahead and t < FOLDED:
                        fold_columns(n + 1, 1 - par, t)
                pool.wait_ge(ca_done, n + 1)
                pool.wait_ge(v_done, (n + 1) * T)
                pool.sem_inc(passed_pool, 1)
                last = ub[:, T - 1, :]
                nc.gpsimd.tensor_scalar(last, last, ca[:, T - 1:T], 0.0, ALU.mult, ALU.add).then_inc(scaled_done, 1)
                pool.wait_ge(scaled_done, n + 1)
                nc.gpsimd.tensor_tensor(xs[:, par, T - 1, :], xs[:, par, T - 1, :], last, ALU.add)\
                    .then_inc(last_x1_done, 1)

            step(0, 0, True, False, True)
            step(1, 1, True, True, True)
            with pool.Fori(0, (B - 4) // 2) as it:
                step(it * 2 + 2, 0, True, True, True)
                step(it * 2 + 3, 1, True, True, True)
            step(B - 2, 0, True, True, True)
            step(B - 1, 1, True, True, False)
            step(B, 0, False, True, False)

        @block.scalar
        def _(act):
            def evac(n, *units):
                for k in units:
                    wait(act, mix_ready, freed(n, k, XT_SLOTS))
                    act.wait_ge(xt_ready, (n - 1) * BACK + k + 1)
                    w = 4 * P if k % UNITS == UNITS - 1 else NB3
                    nc.scalar.activation(xt[:, k % XT_SLOTS, 0:w], p_xt[k % XP_BANKS][:, 0:w], ACT.Copy)\
                      .then_inc(xt_copied, 1)

            def group_mean(n, t):
                act.wait_ge(m1_ready, n * T + t + 1)
                nc.scalar.activation(nm1[:, t:t + 1], p_m1[:, t:t + 1], ACT.Copy, scale=-1.0).then_inc(nm1_done, 1)

            def square1(n, par, t):
                act.wait_ge(x_in[t], (n + 1) * 16)
                act.wait_ge(nm1_done, n * T + t + 1)
                nc.scalar.activation(junk, xs[:, par, t, :], ACT.Square, bias=nm1[:, t:t + 1],
                                     accum_out=sq1[:, t:t + 1]).then_inc(sq1_done, 1)

            def var1(n):
                act.wait_ge(v1_ready, n + 1)
                nc.scalar.activation(ve1[:, :], p_v1, ACT.Identity, bias=eps_s[:, :]).then_inc(ve1_done, 1)

            def group_mean2(n, t):
                act.wait_ge(m2_ready, (n - 1) * T + t + 1)
                nc.scalar.activation(nm2[:, t:t + 1], p_m2[:, t:t + 1], ACT.Copy, scale=-1.0).then_inc(nm2_done, 1)

            def last_sum(n, par):
                act.wait_ge(last_x1_done, n)
                nc.scalar.activation(junk, xs[:, 1 - par, T - 1, :], ACT.Copy, accum_out=s2[:, T - 1:T])\
                    .then_inc(last_sum_done, 1)

            def square2(n, par, t):
                act.wait_ge(nm2_done, (n - 1) * T + t + 1)
                nc.scalar.activation(junk, xs[:, 1 - par, t, :], ACT.Square, bias=nm2[:, t:t + 1],
                                     accum_out=sq2[:, t:t + 1]).then_inc(sq2_done, 1)

            def var2(n, t):
                act.wait_ge(v2_ready, (n - 1) * T + t + 1)
                nc.scalar.activation(ve2[:, t:t + 1], p_v2[:, t:t + 1], ACT.Identity, bias=eps_s[:, :])\
                    .then_inc(ve2_done, 1)

            def step(n, par, front, back, ahead):
                if back:
                    act.wait_ge(sq1_done, (n + 1) * T if front else n * T)
                    for t in range(T - 1):
                        group_mean2(n, t)
                        if t > 0:
                            var2(n, t - 1)
                            act.wait_ge(sq2_done, (n - 1) * T + t)
                        if t == 2:
                            evac(n, 0, 1)
                        square2(n, par, t)
                    evac(n, 2)
                    var2(n, T - 2)
                    evac(n, 3)
                    act.wait_ge(sq2_done, n * T - 1)
                    last_sum(n, par)
                    evac(n, 4)
                    group_mean2(n, T - 1)
                    evac(n, 5)
                if front:
                    act.wait_ge(fm_ready, n + 1)
                    nc.scalar.activation(fm[:, :], p_fm, ACT.Copy).then_inc(fm_done, 1)
                if back:
                    evac(n, 6, 7, 8)
                if front:
                    act.wait_ge(hb_done, HB * (n + 1))
                    for d in (1, 0):
                        for t in range(T):
                            k = d * T + t
                            nc.scalar.activation(th[:, d, t, :], ff[:, 0, d, t, :], ACT.Tanh,
                                                 scale=hv[:, 1, k:k + 1], bias=hv[:, 3, k:k + 1]).then_inc(th_done, 1)
                        if back:
                            evac(n, 10 - d)
                if back:
                    if not front:
                        evac(n, 9, 10)
                    act.wait_ge(last_sum_done, n)
                    square2(n, par, T - 1)
                    evac(n, 11, 12)
                    var2(n, T - 1)
                    evac(n, *range(13, BACK))
                if not front:
                    return
                m, mpar = n + 1, 1 - par
                if ahead:
                    group_mean(m, 0)
                    group_mean(m, 1)
                    act.wait_ge(rowsum_done, m * T + FOLDED)
                    square1(m, mpar, 0)
                act.wait_ge(ym_ready, n + 1)
                nc.scalar.activation(ym[:, :], p_ym, ACT.Copy, scale=float(P * H) / (C * L)).then_inc(ym_done, 1)
                if ahead:
                    act.wait_ge(sq1_done, m * T + 1)
                    square1(m, mpar, 1)
                    group_mean(m, 2)
                act.wait_ge(ynt_ready, n + 1)
                nc.scalar.activation(ynt, p_ynt, ACT.Copy).then_inc(ynt_done, 1)
                if ahead:
                    act.wait_ge(sq1_done, m * T + 2)
                    square1(m, mpar, 2)
                act.wait_ge(att_done, ATT * n + 3)
                nc.scalar.activation(ee[:, 0, :, :], at[:, :, :], ACT.Exp).then_inc(exp_done, 1)
                if ahead:
                    group_mean(m, 3)
                act.wait_ge(att_done, ATT * n + 7)
                nc.scalar.activation(tc[:, :], oo[:, :], ACT.Tanh, scale=0.5).then_inc(tc_done, 1)
                if ahead:
                    act.wait_ge(sq1_done, m * T + 3)
                    square1(m, mpar, 3)
                    var1(m)

            act.wait_ge(zeros_set, 1)
            act.wait_ge(psum_clear, 1)
            for t in range(T):
                group_mean(0, t)
                wait(act, sq1_done, t)
                square1(0, 0, t)
            var1(0)
            step(0, 0, True, False, True)
            step(1, 1, True, True, True)
            with act.Fori(0, (B - 4) // 2) as it:
                step(it * 2 + 2, 0, True, True, True)
                step(it * 2 + 3, 1, True, True, True)
            step(B - 2, 0, True, True, True)
            step(B - 1, 1, True, True, False)
            step(B, 0, False, True, False)

        @block.tensor
        def _(pe):
            pe.wait_ge(psum_clear, 1)
            pe.wait_ge(zeros_set, 1)
            pe.wait_ge(consts_in, 16 * 13)
            pe.wait_ge(consts_set, 1)

            def colsum(n, par, t, part=None):
                groups = H // 4
                first, end = (0, groups) if part is None else ((0, groups // 2), (groups // 2, groups))[part]
                if first == 0:
                    pe.wait_ge(x_in[t], (n + 1) * 16)
                    wait(pe, added, (n - 2) * BACK + BACK - T + t + 1)
                v = xs[:, par, t, :].rearrange("p (g f) -> p g f", f=4 * W)
                for g in range(first, end):
                    mm = pe.matmul(p_col[t][:, 0:4 * W], ident[:, :], v[:, g, :],
                                   start=(g == 0), stop=(g == groups - 1))
                if end == groups:
                    mm.then_inc(colsum_ready, 1)

            def group_mean(n, t):
                pe.wait_ge(chsum_done, n * T + t + 1)
                wait(pe, nm1_done, n * T + t)
                wait(pe, ym_done, n if t > 1 else n - 1)
                pe.matmul(p_m1[:, t:t + 1], gmean[:, :], chs[:, t:t + 1], start=True, stop=True).then_inc(m1_ready, 1)

            def var1(n):
                pe.wait_ge(sq1_done, (n + 1) * T)
                pe.matmul(p_v1, gmean[:, :], sq1[:, :], start=True, stop=True).then_inc(v1_ready, 1)

            def mean(n, t):
                if t < T - 1:
                    pe.wait_ge(x1_done, (n - 1) * (T - 1) + t + 1)
                else:
                    pe.wait_ge(last_sum_done, n)
                wait(pe, nm2_done, (n - 1) * T + t)
                wait(pe, ve2_done, (n - 1) * T + (t if t == T - 1 else max(t - 1, 0)))
                pe.matmul(p_m2[:, t:t + 1], gmean[:, :], s2[:, t:t + 1], start=True, stop=True).then_inc(m2_ready, 1)

            def var(n, t):
                pe.wait_ge(sq2_done, (n - 1) * T + t + 1)
                pe.wait_ge(nm2_done, (n - 1) * T + (T if t == T - 1 else min(t + 2, T - 1)))
                wait(pe, ve2_done, (n - 1) * T + t)
                pe.matmul(p_v2[:, t:t + 1], gmean[:, :], sq2[:, t:t + 1], start=True, stop=True).then_inc(v2_ready, 1)

            def turn(n, k):
                t, j = divmod(k, UNITS)
                if j == 0:
                    pe.wait_ge(xn_done, (n - 1) * XN * T + XN * t + 1)
                if j >= COLS:
                    pe.wait_ge(xn_done, (n - 1) * XN * T + XN * t + (2 if j == COLS else XN))
                wait(pe, xt_copied, freed(n, k, XP_BANKS))
                if k < 2:
                    wait(pe, att_done, ATT * (n - 1) + 4)
                ps = p_xt[k % XP_BANKS]
                for b in range(3):
                    mm = pe.transpose(ps[:, b * P:(b + 1) * P], ub[:, t, j * NB3 + b * P:j * NB3 + (b + 1) * P],
                                      ident[:, :])
                if j == UNITS - 1:
                    mm = pe.transpose(ps[0:64, 3 * P:4 * P], ub[:, t, HW - 64:HW], ident[:, :])
                mm.then_inc(xt_ready, 1)

            def mix(n, k, front):
                t, j = divmod(k, UNITS)
                kind = kind_of(j)
                s = k % XT_SLOTS
                ps = p_y[k % Y_BANKS]
                wait(pe, added, freed(n, k, Y_BANKS))
                if front and k < T:
                    pe.wait_ge(colsum_read, n * T + k + 1)
                rhs = bpat[:, kind, :].unsqueeze(1).broadcast_to([P, 3, P])
                pe.matmul(ps[:, 0:NB3], heads[:, t, :], rhs, start=True, stop=False, skip_group_check=True)
                if j == UNITS - 1:
                    pe.matmul(ps[:, NB3:NB3 + 64], heads[:, t, :], bpat[:, CORNERS, 0:64], start=False, stop=False,
                              skip_group_check=True)
                pe.wait_ge(xt_copied, (n - 1) * BACK + k + 1)
                nb = 4 if j == UNITS - 1 else 3
                for b in range(nb):
                    for q in range(HPT):
                        rows = slice(HD * q, HD * (q + 1))
                        cols = slice(b * P + HD * q, b * P + HD * (q + 1))
                        if b == 3:
                            o, xb, wb = ps[rows, NB3:NB3 + 64], xt[0:64, s, cols], wcor[:, t * HPT + q, :]
                        else:
                            o, xb, wb = ps[rows, b * P:(b + 1) * P], xt[:, s, cols], wwin[:, kind, t * HPT + q, :]
                        mm = pe.matmul(o, xb, wb, start=False, stop=(b == nb - 1), skip_group_check=True,
                                       tile_position=(0, HD * q))
                mm.then_inc(mix_ready, 1)

            def step(n, par, front, back, ahead):
                if back:
                    mean(n, 2)
                    var(n, 1)
                    turn(n, 0)
                for k in range(BACK):
                    if back:
                        if k < BACK - 1:
                            turn(n, k + 1)
                        mix(n, k, front)
                        if k == 1:
                            var(n, 2)
                        if k == 3:
                            mean(n, 3)
                    if front and k == 4:
                        pe.wait_ge(fstat_done, n + 1)
                        pe.matmul(p_fm, ones_h[:, :], fs[:, :], start=True, stop=True).then_inc(fm_ready, 1)
                    if back and k == 11:
                        var(n, 3)
                if not front:
                    return
                m, mpar = n + 1, 1 - par
                if ahead:
                    group_mean(m, 0)
                    colsum(m, mpar, 0)
                    group_mean(m, 1)
                    colsum(m, mpar, 1)
                    pe.wait_ge(nm1_done, m * T + 2)
                pe.wait_ge(ystat_done, n + 1)
                pe.matmul(p_ym, ones_h[:, :], ys[:, :], start=True, stop=True).then_inc(ym_ready, 1)
                if ahead:
                    colsum(m, mpar, 2, 0)
                    group_mean(m, 2)
                wait(pe, xt_copied, n * BACK)
                pe.wait_ge(yn_done, T * (n + 1))
                pe.sem_inc(passed_pe, 1)
                for t in range(T):
                    mm = pe.transpose(p_ynt[:, t * P:(t + 1) * P], y[:, t, :], ident[:, :])
                mm.then_inc(ynt_ready, 1)
                pe.wait_ge(ynt_done, n + 1)
                pe.sem_inc(passed_pe, 1)
                for t in range(T):
                    for q in range(HPT):
                        rows = slice(HD * q, HD * (q + 1))
                        cols = slice(t * P + HD * q, t * P + HD * (q + 1))
                        pe.matmul(p_gram[rows, HD * t:HD * (t + 1)], ynt[:, cols], ynt[:, cols],
                                  start=True, stop=True, tile_position=(0, HD * q))
                for q in range(HPT):
                    rows = slice(HD * q, HD * (q + 1))
                    v = ynt.rearrange("p (t q c) -> p t q c", t=T, q=HPT)[:, :, q, :]
                    mm = pe.matmul(p_vb[rows, :], ones_l[:, :], v, start=True, stop=True, tile_position=(0, HD * q))
                mm.then_inc(gram_ready, 1)
                if ahead:
                    group_mean(m, 3)
                    colsum(m, mpar, 2, 1)
                    colsum(m, mpar, 3, 0)
                    var1(m)
                mean(m, 0)
                if ahead:
                    colsum(m, mpar, 3, 1)
                mean(m, 1)
                var(m, 0)

            for t in range(T):
                colsum(0, 0, t)
            for t in range(T):
                group_mean(0, t)
            var1(0)
            step(0, 0, True, False, True)
            pe.wait_ge(wwin_in, 32)
            step(1, 1, True, True, True)
            with pe.Fori(0, (B - 4) // 2) as it:
                step(it * 2 + 2, 0, True, True, True)
                step(it * 2 + 3, 1, True, True, True)
            step(B - 2, 0, True, True, True)
            step(B - 1, 1, True, True, False)
            step(B, 0, False, True, False)

        @block.vector
        def _(dve):
            v = nc.vector
            for ps in p_xt + p_y + [p_front, p_back]:
                last = v.memset(ps[:, :], 0.0)
            last.then_inc(psum_clear, 1)
            dve.wait_ge(zeros_set, 1)
            dve.wait_ge(b_in, 16 * 4)
            v.memset(bpat[:, :, :], 0.0).then_inc(split, 1)
            v.tensor_copy(heads[:, :, :].rearrange("p t c -> p (t c)"), ub[:, 1, 0:T * P])
            bsrc = ub[:, 0, 0:KINDS * P]
            part = junk[:, 0:KINDS * P]
            dve.wait_ge(split, 1)
            done = 1
            for k in range(3):
                v.tensor_copy(part, bsrc).then_inc(split, 1)
                done += 1
                dve.wait_ge(split, done)
                v.tensor_copy(bpat[32 * k:32 * (k + 1), :, :].rearrange("p k c -> p (k c)"),
                              part[32 * k:32 * (k + 1), :])
                v.tensor_tensor(bsrc, bsrc, part, ALU.subtract).then_inc(split, 1)
                done += 1
                dve.wait_ge(split, done)
            dve.wait_ge(consts_in, 16 * 13)
            for t in range(T):
                v.tensor_scalar(wqk_s[:, t, :], wqk_s[:, t, :], gmb[:, 6, t:t + 1], float(HD) ** -0.5, ALU.mult, ALU.mult)
            v.tensor_scalar(wv_s[:, :, :], wv_s[:, :, :], 1.0 / L, None, ALU.mult)
            v.tensor_scalar(gmb[:, 0:4, :], gmb[:, 0:4, :], 0.5, None, ALU.mult).then_inc(consts_set, 1)
            dve.wait_ge(consts_set, 1)

            def bcast(ap, w):
                return ap.unsqueeze(2).broadcast_to([P, ap.shape[1], w])

            def add_units(n, par, *units):
                for k in units:
                    t, j = divmod(k, UNITS)
                    ps = p_y[k % Y_BANKS]
                    dve.wait_ge(mix_ready, (n - 1) * BACK + k + 1)
                    if j < COLS:
                        m = image(xs[:, 1 - par, t, :])[:, SHIFT:SHIFT + IN, SHIFT + WS * j:SHIFT + WS * (j + 1)]
                        pairs = [(m, ps[:, 0:NB3].rearrange("p (h c) -> p h c", c=WS))]
                    else:
                        im = image_pieces(xs[:, 1 - par, t, :])
                        pairs = zip(im[1:2], sides_in(ps)) if j == COLS else zip(im[2:], ends_in(ps))
                    for m, product in pairs:
                        ins = v.tensor_tensor(m, product, m, ALU.add)
                    ins.then_inc(added, 1)

            def rowsum(n, par, t):
                if t < FOLDED and not (isinstance(n, int) and n == 0):
                    dve.wait_ge(fold_done, (n - 1) * FOLDED + t + 1)
                    src = fold
                else:
                    dve.wait_ge(x_in[t], (n + 1) * 16)
                    src = image(xs[:, par, t, :])
                v.tensor_reduce(rs[:, 0, t, :], src, AX.X, ALU.add).then_inc(rowsum_done, 1)

            def colsum_read_out(n, t):
                dve.wait_ge(colsum_ready, n * T + t + 1)
                v.tensor_reduce(rs[:, 1, t, :], p_col[t][:, 0:4 * W].rearrange("p (f w) -> p w f", w=W),
                                AX.X, ALU.add).then_inc(colsum_read, 1)

            def channel_sum(n, t):
                dve.wait_ge(rowsum_done, n * T + t + 1)
                v.tensor_reduce(chs[:, t:t + 1], rs[:, 0, t, :], AX.X, ALU.add).then_inc(chsum_done, 1)

            def convs(n, par, back):
                dve.wait_ge(nm1_done, (n + 1) * T)
                dve.wait_ge(colsum_read, (n + 1) * T)
                for d in range(2):
                    v.scalar_tensor_tensor(xp[:, d, :, PAD:PAD + H], bcast(nm1[:, :], H), float(H), rs[:, d, :, :],
                                           ALU.mult, ALU.add).then_inc(centred, 1)
                dve.wait_ge(centred, 2 * (n + 1))
                count, last = 0, {}
                for tap in range(max(KS)):
                    for d in range(2):
                        for t in range(T):
                            if tap >= KS[t]:
                                continue
                            src = xp[:, d, t, PAD + tap - KS[t] // 2:PAD + tap - KS[t] // 2 + H]
                            wi = sum(KS[:t]) + tap
                            dst = ff[:, 0, d, t, :]
                            if tap == 0:
                                ins = v.tensor_scalar(dst, src, wc[:, d, wi:wi + 1], None, ALU.mult)
                            else:
                                dve.wait_ge(tap_done, TAPS2 * n + last[d, t])
                                ins = v.scalar_tensor_tensor(dst, src, wc[:, d, wi:wi + 1], dst, ALU.mult, ALU.add)
                            ins.then_inc(tap_done, 1)
                            count += 1
                            last[d, t] = count
                    if back and tap == 4:
                        add_units(n, par, 0)
                assert count == TAPS2

            def conv_stats(n):
                dve.wait_ge(r1_done, n + 1)
                dve.wait_ge(tap_done, TAPS2 * (n + 1))
                for d in range(2):
                    v.scalar_tensor_tensor(ff[:, 0, d, :, :], ff[:, 0, d, :, :], 1.0 / H, bcast(r1[:, :], H),
                                           ALU.mult, ALU.mult).then_inc(f_done, 1)
                dve.wait_ge(f_done, F3 * n + 2)
                f = ff[:, 0, :, :, :].rearrange("p d t h -> p (d t) h")
                v.tensor_tensor(f, f, bcast(bc[:, :, :].rearrange("p d t -> p (d t)"), H), ALU.add).then_inc(f_done, 1)
                dve.wait_ge(f_done, F3 * n + 3)
                v.tensor_tensor(ff[:, 1, :, :, :], ff[:, 0, :, :, :], ff[:, 0, :, :, :], ALU.mult).then_inc(f_done, 1)
                dve.wait_ge(f_done, F3 * (n + 1))
                v.tensor_reduce(fs[:, :], ff[:, :, :, :, :].rearrange("p a d t h -> p (a d t) h"), AX.X, ALU.add)\
                 .then_inc(fstat_done, 1)

            def gate_var(n):
                dve.wait_ge(fm_done, n + 1)
                v.tensor_tensor(hv[:, 0, :], fm[:, 0:8], fm[:, 0:8], ALU.mult).then_inc(gv, 1)
                dve.wait_ge(gv, 2 * n + 1)
                v.tensor_tensor(hv[:, 0, :], fm[:, 8:16], hv[:, 0, :], ALU.subtract).then_inc(gv, 1)
                dve.wait_ge(gv, 2 * n + 2)
                v.tensor_scalar(hv[:, 2, :], hv[:, 0, :], 0.0, EPS, ALU.max, ALU.add).then_inc(vh_done, 1)

            def gate_affine(n):
                dve.wait_ge(rh_done, n + 1)
                v.tensor_tensor(hv[:, 1, :], rh[:, :], gmb[:, 0:2, :].rearrange("p a t -> p (a t)"), ALU.mult)\
                 .then_inc(hb_done, 1)
                dve.wait_ge(hb_done, HB * n + 1)
                v.tensor_tensor(hv[:, 3, :], fm[:, 0:8], hv[:, 1, :], ALU.mult).then_inc(hb_done, 1)
                dve.wait_ge(hb_done, HB * n + 2)
                v.tensor_tensor(hv[:, 3, :], gmb[:, 2:4, :].rearrange("p a t -> p (a t)"), hv[:, 3, :],
                                ALU.subtract).then_inc(hb_done, 1)

            def column_gate(n):
                dve.wait_ge(th_done, 2 * T * n + T)
                v.tensor_scalar(th[:, 1, :, :], th[:, 1, :, :], 0.25, 0.25, ALU.mult, ALU.add).then_inc(gate_done, 1)

            def row_gate(n):
                dve.wait_ge(th_done, 2 * T * (n + 1))
                v.scalar_tensor_tensor(th[:, 0, :, :], th[:, 0, :, :], 1.0, bcast(r1[:, :], H), ALU.add, ALU.mult)\
                 .then_inc(gate_done, 1)

            def gate_columns(n, par, t):
                if not (isinstance(n, int) and n == 0):
                    dve.wait_ge(xt_ready, (n - 1) * BACK + UNITS * (t + 1))
                g = th[:, 1, t, :].unsqueeze(1).broadcast_to([P, H, W])
                v.scalar_tensor_tensor(image(ub[:, t, :]), image(xs[:, par, t, :]), nm1[:, t:t + 1], g,
                                       ALU.add, ALU.mult).then_inc(u_done, 1)

            def pool_columns(n, t):
                dve.wait_ge(u_done, n * T + t + 1)
                wait(dve, y_done, n * T + t)
                v.tensor_reduce(pm[:, :], ub[:, t, :].rearrange("p (k w) -> p k w", w=WIN), AX.X, ALU.max)\
                 .then_inc(wmax_done, 1)

            def pool_rows(n, par, t, *between):
                q3 = pm[:, :].rearrange("p (h k) -> p h k", k=NW)
                dve.wait_ge(wmax_done, n * T + t + 1)
                if t == 0:
                    dve.wait_ge(gate_done, 2 * (n + 1))
                v.tensor_tensor(q3, q3, bcast(th[:, 0, t, :], NW), ALU.mult).then_inc(wgate_done, 1)
                add_units(n, par, *between)
                dve.wait_ge(wgate_done, n * T + t + 1)
                v.tensor_reduce(y[:, t, :], pm[:, :].rearrange("p (a r k) -> p a k r", r=WIN, k=NW), AX.X, ALU.max)\
                 .then_inc(y_done, 1)

            def pooled_sums(n):
                dve.wait_ge(y_done, T * (n + 1))
                yf = y[:, :, :].rearrange("p t l -> p (t l)")
                v.tensor_reduce(ys[:, 0:1], yf, AX.X, ALU.add)
                v.scalar_tensor_tensor(yj, yf, 1.0, yf, ALU.mult, ALU.mult, accum_out=ys[:, 1:2])\
                 .then_inc(ystat_done, 1)

            def pooled_var(n):
                dve.wait_ge(ym_done, n + 1)
                v.tensor_tensor(yv[:, 0:1], ym[:, 0:1], ym[:, 0:1], ALU.mult).then_inc(yq, 1)
                dve.wait_ge(yq, 5 * n + 1)
                v.tensor_tensor(yv[:, 0:1], ym[:, 1:2], yv[:, 0:1], ALU.subtract).then_inc(yq, 1)
                dve.wait_ge(yq, 5 * n + 2)
                v.tensor_scalar(yv[:, 1:2], yv[:, 0:1], 0.0, EPS, ALU.max, ALU.add).then_inc(yvar_done, 1)

            def pooled_norm(n):
                dve.wait_ge(ry_done, n + 1)
                v.tensor_scalar(ab[:, 0, :], gmb[:, 4, :], ry[:, 0:1], None, ALU.mult).then_inc(yq, 1)
                dve.wait_ge(yq, 5 * n + 3)
                v.tensor_scalar(ab[:, 1, :], ab[:, 0, :], ym[:, 0:1], None, ALU.mult).then_inc(yq, 1)
                dve.wait_ge(yq, 5 * n + 4)
                v.tensor_tensor(ab[:, 2, :], gmb[:, 5, :], ab[:, 1, :], ALU.subtract).then_inc(yq, 1)
                dve.wait_ge(yq, 5 * n + 5)
                for t in range(T):
                    v.tensor_scalar(y[:, t, :], y[:, t, :], ab[:, 0, t:t + 1], ab[:, 2, t:t + 1],
                                    ALU.mult, ALU.add).then_inc(yn_done, 1)

            def logits(n):
                g = p_gram.rearrange("p (t c) -> p t c", t=T)
                vb = p_vb.rearrange("p (t c) -> p t c", t=T)
                dve.wait_ge(gram_ready, n + 1)
                v.tensor_tensor(at[:, :, :], g, wqk_s[:, :, :], ALU.mult).then_inc(att_done, 1)
                dve.wait_ge(att_done, ATT * n + 1)
                v.tensor_reduce(mx[:, :], at[:, :, :], AX.X, ALU.max).then_inc(att_done, 1)
                dve.wait_ge(att_done, ATT * n + 2)
                v.tensor_tensor(at[:, :, :], at[:, :, :], bcast(mx[:, :], HD), ALU.subtract).then_inc(att_done, 1)
                v.tensor_tensor(ee[:, 1, :, :], vb, wv_s[:, :, :], ALU.mult).then_inc(att_done, 1)

            def attend(n):
                dve.wait_ge(exp_done, n + 1)
                dve.wait_ge(att_done, ATT * n + 4)
                v.tensor_tensor(ee[:, 1, :, :], ee[:, 0, :, :], ee[:, 1, :, :], ALU.mult).then_inc(att_done, 1)
                dve.wait_ge(att_done, ATT * n + 5)
                v.tensor_reduce(ss[:, :, :].rearrange("p a t -> p (a t)"),
                                ee[:, :, :, :].rearrange("p a t c -> p (a t) c"), AX.X, ALU.add).then_inc(att_done, 1)
                dve.wait_ge(att_done, ATT * n + 6)
                v.reciprocal(rd[:, :], ss[:, 0, :]).then_inc(rdone, 1)
                dve.wait_ge(rdone, n + 1)
                v.tensor_tensor(oo[:, :], ss[:, 1, :], rd[:, :], ALU.mult).then_inc(att_done, 1)

            def channel_gate(n):
                dve.wait_ge(tc_done, n + 1)
                v.tensor_scalar(ca[:, :], tc[:, :], 0.5, 0.5, ALU.mult, ALU.add).then_inc(ca_done, 1)
                dve.wait_ge(ca_done, n + 1)

            def first_out(n, par, t):
                dve.wait_ge(v_done, n * T + t + 1)
                v.scalar_tensor_tensor(xs[:, par, t, :], ub[:, t, :], ca[:, t:t + 1], xs[:, par, t, :],
                                       ALU.mult, ALU.add, accum_out=s2[:, t:t + 1]).then_inc(x1_done, 1)

            def step(n, par, front, back, ahead):
                def units(*ks):
                    if back:
                        add_units(n, par, *ks)

                if not front:
                    units(*range(BACK))
                    return
                convs(n, par, back)
                units(1, 2)
                conv_stats(n)
                units(3, 4)
                gate_var(n)
                units(5, 6)
                gate_affine(n)
                units(7, 8)
                column_gate(n)
                m, mpar = n + 1, 1 - par
                dve.wait_ge(gate_done, 2 * n + 1)

                def sums(t, *between):
                    if ahead:
                        rowsum(m, mpar, t)
                    units(*between)
                    if ahead:
                        channel_sum(m, t)

                def rows(t, *between):
                    pool_rows(n, par, t, *(between if back else ()))

                def column_sums(t):
                    if ahead:
                        colsum_read_out(m, t)

                gate_columns(n, par, 0)
                units(9, 10, 11)
                row_gate(n)
                pool_columns(n, 0)
                units(12, 13)
                rows(0, 14)
                units(15, 16)
                gate_columns(n, par, 1)
                units(17, 18)
                pool_columns(n, 1)
                units(19, 20)
                sums(0, 21)
                rows(1, 22)
                gate_columns(n, par, 2)
                units(23, 24)
                pool_columns(n, 2)
                units(25, 26)
                rows(2, 27)
                units(28)
                sums(1, 29)
                gate_columns(n, par, 3)
                units(30, 31)
                pool_columns(n, 3)
                rows(3)
                pooled_sums(n)
                pooled_var(n)
                column_sums(0)
                sums(2)
                pooled_norm(n)
                sums(3)
                column_sums(1)
                logits(n)
                attend(n)
                channel_gate(n)
                for t in range(T - 1):
                    first_out(n, par, t)
                    if t == 1:
                        column_sums(2)
                column_sums(3)

            for t in range(T):
                rowsum(0, 0, t)
                colsum_read_out(0, t)
                channel_sum(0, t)
            step(0, 0, True, False, True)
            step(1, 1, True, True, True)
            with dve.Fori(0, (B - 4) // 2) as it:
                step(it * 2 + 2, 0, True, True, True)
                step(it * 2 + 3, 1, True, True, True)
            step(B - 2, 0, True, True, True)
            step(B - 1, 1, True, True, False)
            step(B, 0, False, True, False)


def window_weights(w):
    out = np.zeros((P, KINDS, HEADS, P), w.dtype)
    for kind in range(KINDS):
        places = block_positions(kind)
        for win in range(4):
            at = [p for p, (v, _) in enumerate(places) if v == win]
            if at:
                pos = [places[p][1] for p in at]
                out[np.array(at)[:, None], kind, :, np.array(at)[None, :]] = w[:, pos][:, :, pos].transpose(2, 1, 0)
    return out


def window_bias(b):
    out = np.zeros((HEADS, KINDS, P), b.dtype)
    for kind in range(KINDS):
        places = block_positions(kind)
        out[:, kind, :len(places)] = b[:, [pos for _, pos in places]]
    return out.reshape(HEADS, KINDS * P)


def shape_constants():
    ident = np.eye(P, dtype=np.float32)
    gmean = np.kron(np.eye(P // GROUP), np.full((GROUP, GROUP), 1.0 / (GROUP * HW))).astype(np.float32)
    heads = np.zeros((P, T, P), np.float32)
    for part in range(3):
        for head in range(HEADS):
            t, q = divmod(head, HPT)
            heads[32 * part + head, t, HD * q:HD * (q + 1)] = 1.0
    return ident, gmean, heads.reshape(P, T * P)


def kernel(**inputs):
    import concourse.bacc as bacc
    from concourse.bass_utils import run_bass_kernel_spmd as run

    a = {k: np.asarray(v) for k, v in inputs.items()}
    g = {k[len("L0_conv_"):]: v for k, v in a.items() if k.startswith("L0_conv_")}

    def per_tile(names):
        return np.concatenate([g[k].reshape(P, -1) for k in names], axis=1)

    hs, ws = ("lh", "sh", "mh", "gh"), ("lw", "sw", "mw", "gw")
    ident, gmean, heads = shape_constants()
    arrays = {
        "x": np.ascontiguousarray(a["x"]).reshape(B, C, HW),
        "w_conv": np.ascontiguousarray(np.stack([per_tile(["w_" + k for k in hs]), per_tile(["w_" + k for k in ws])], 1)),
        "b_conv": np.ascontiguousarray(np.stack([per_tile(["b_" + k for k in hs]), per_tile(["b_" + k for k in ws])], 1)),
        "gam": np.ascontiguousarray(np.stack([g[k].reshape(T, P).T for k in (
            "gn_h_g", "gn_w_g", "gn_h_b", "gn_w_b", "gn_g", "gn_b", "wq")], 1)),
        "wk": np.ascontiguousarray(g["wk"]),
        "wv": np.ascontiguousarray(g["wv"]),
        "w_win": window_weights(a["L1_conv_w"]),
        "b_win": window_bias(a["L1_conv_b"]),
        "ident": ident,
        "gmean": gmean,
        "heads": heads,
    }
    nc = bacc.Bacc("TRN2", target_bir_lowering=False, num_devices=1)
    args = [nc.dram_tensor(k + "_in", v.shape, mybir.dt.from_np(v.dtype), kind="ExternalInput").ap() for k, v in arrays.items()]
    out = nc.dram_tensor("out", (B, C, HW), F32, kind="ExternalOutput").ap()
    build(nc, *args, out)
    got = run(nc, [{k + "_in": v for k, v in arrays.items()}], core_ids=[0]).results[0]["out"]
    return got.reshape(B, C, H, W)
```

```python
import numpy as np
from contextlib import ExitStack

import concourse.bass as bass
from concourse import mybir

F32 = mybir.dt.float32
BF16 = mybir.dt.bfloat16
ALU = mybir.AluOpType
ACT = mybir.ActivationFunctionType
AX = mybir.AxisListType

B, C, H, W = 32, 512, 56, 56
P = 128
T = C // P
HW = H * W
KS = (3, 5, 7, 9)
NTAPS = sum(KS)
PADW = 64
PAD = 4
WIN = 7
NW = H // WIN
L = NW * NW
HEADS, HD = 16, 32
HPT = P // HD
WS, SHIFT = 8, 4
KINDS = 4
INTERIOR, SIDES, ENDS, CORNERS = range(KINDS)
COLS = 6
UNITS = COLS + 2
IN = H - 2 * SHIFT
NB3 = 3 * P
XT_SLOTS = 3
XP_BANKS = 2
Y_BANKS = 4
FOLDED = 2
PLACED = (18, 25, 27)
ADDED = tuple(k for k in range(UNITS * T) if k not in PLACED)
assert all(k % UNITS < UNITS - Y_BANKS and k % UNITS < COLS for k in PLACED)
GROUP = 16
EPS = 1e-5


def block_positions(kind):
    out = []
    for w in range(2 if kind != CORNERS else 1):
        if kind == INTERIOR:
            out += [(w, r * WS + c) for r in range(WS) for c in range(WS)]
        elif kind == SIDES:
            out += [(2 * w + side, r * WS + SHIFT * (1 - side) + c)
                    for r in range(WS) for side in range(2) for c in range(SHIFT)]
        elif kind == ENDS:
            out += [(2 * w + end, (SHIFT * (1 - end) + r) * WS + c)
                    for end in range(2) for r in range(SHIFT) for c in range(WS)]
        else:
            out += [(2 * end + side, (SHIFT * (1 - end) + r) * WS + SHIFT * (1 - side) + c)
                    for end in range(2) for r in range(SHIFT) for side in range(2) for c in range(SHIFT)]
    return out


def build(nc, x, w_conv, b_conv, gam, wk, wv, w_win, b_win, ident_d, gmean_d, heads_d, out):
    with ExitStack() as ctx:
        def sb(name, shape, dt=F32):
            return ctx.enter_context(nc.sbuf_tensor(name, shape, dt))

        def pb(name):
            return ctx.enter_context(nc.psum_tensor(name, [P, 512], F32))

        def sem(name):
            return ctx.enter_context(nc.semaphore(name))

        ident = sb("ident", [P, P])
        gmean = sb("gmean", [P, P])
        ones_h = sb("ones_h", [P, P])
        ones_l = sb("ones_l", [L, HD])
        heads = sb("heads", [P, T, P], BF16)
        bpat = sb("bpat", [P, KINDS, P], BF16)
        wwin = sb("wwin", [P, KINDS - 1, HEADS, P])
        wcor = sb("wcor", [2 * HD, HEADS, 2 * HD])
        wc = sb("wc", [P, 2, NTAPS])
        bc = sb("bc", [P, 2, T])
        gmb = sb("gmb", [P, 7, T])
        wqk_s = sb("wqk_s", [P, T, HD])
        wv_s = sb("wv_s", [P, T, HD])
        eps_s = sb("eps_s", [P, 1])
        mhalf = sb("mhalf", [P, 8])
        xs = sb("xs", [P, 2, T, HW])
        ub = sb("ub", [P, T, HW])
        spare = sb("spare", [P, HW // 2])
        junk = spare[:, :].bitcast(BF16)
        fold = spare[:, :].rearrange("p (h w) -> p h w", w=W // 2)
        xt = sb("xt", [P, XT_SLOTS, 4 * P])
        ynt = xt[0:L, 0, :]
        yj = xt[:, 1, 0:T * L]
        rs = sb("rs", [P, 2, T, H])
        chs = sb("chs", [P, T])
        nm1 = sb("nm1", [P, T])
        sq1 = sb("sq1", [P, T])
        ve1 = sb("ve1", [P, T])
        r1 = sb("r1", [P, T])
        xp = sb("xp", [P, 2, T, PADW])
        ff = sb("ff", [P, 2, 2, T, H])
        fs = sb("fs", [P, 16])
        fm = sb("fm", [P, 16])
        hv = sb("hv", [P, 4, 8])
        rh = sb("rh", [P, 8])
        th = sb("th", [P, 2, T, H])
        pm = sb("pm", [P, H * NW])
        y = sb("y", [P, T, L])
        ys = sb("ys", [P, 2])
        ym = sb("ym", [P, 2])
        yv = sb("yv", [P, 2])
        ry = sb("ry", [P, 1])
        ab = sb("ab", [P, 3, T])
        at = sb("at", [P, T, HD])
        mx = sb("mx", [P, T])
        ee = sb("ee", [P, 2, T, HD])
        ss = sb("ss", [P, 2, T])
        rd = sb("rd", [P, T])
        oo = sb("oo", [P, T])
        tc = sb("tc", [P, T])
        ca = sb("ca", [P, T])
        s2 = sb("s2", [P, T])
        nm2 = sb("nm2", [P, T])
        sq2 = sb("sq2", [P, T])
        ve2 = sb("ve2", [P, T])
        r2 = sb("r2", [P, T])
        nmr2 = sb("nmr2", [P, T])

        p_xt = [pb(f"p_xt{i}") for i in range(XP_BANKS)]
        p_y = [pb(f"p_y{i}") for i in range(Y_BANKS)]
        p_col = p_y
        p_front, p_back = pb("p_front"), pb("p_back")
        p_ynt = p_xt[0][0:L, :]
        p_gram, p_vb = p_xt[1][:, 0:P], p_xt[1][:, P:2 * P]
        p_m1, p_v1, p_fm, p_ym = p_front[:, 0:T], p_front[:, 8:12], p_front[:, 16:32], p_front[:, 32:34]
        p_m2, p_v2 = p_back[:, 0:4], p_back[:, 8:12]

        matrices_in, consts_in, wwin_in, b_in = sem("matrices_in"), sem("consts_in"), sem("wwin_in"), sem("b_in")
        psum_clear, zeros_set, consts_set = sem("psum_clear"), sem("zeros_set"), sem("consts_set")
        split = sem("split")
        x_in = [sem(f"x_in{t}") for t in range(T)]
        out_done = [sem(f"out_done{t}") for t in range(T)]
        rowsum_done, colsum_ready, colsum_read, chsum_done = (
            sem("rowsum_done"), sem("colsum_ready"), sem("colsum_read"), sem("chsum_done"))
        m1_ready, nm1_done, sq1_done, v1_ready, ve1_done, r1_done = (
            sem("m1_ready"), sem("nm1_done"), sem("sq1_done"), sem("v1_ready"), sem("ve1_done"), sem("r1_done"))
        centred, tap_done, f_done, fstat_done = sem("centred"), sem("tap_done"), sem("f_done"), sem("fstat_done")
        fm_ready, fm_done, vh_done, rh_done, hb_done, th_done, gate_done = (
            sem("fm_ready"), sem("fm_done"), sem("vh_done"), sem("rh_done"), sem("hb_done"), sem("th_done"),
            sem("gate_done"))
        u_done, fold_done, wmax_done, wgate_done, y_done, v_done = (
            sem("u_done"), sem("fold_done"), sem("wmax_done"), sem("wgate_done"), sem("y_done"), sem("v_done"))
        ystat_done, ym_ready, ym_done, yvar_done, ry_done, yn_done = (
            sem("ystat_done"), sem("ym_ready"), sem("ym_done"), sem("yvar_done"), sem("ry_done"), sem("yn_done"))
        (ynt_ready, ynt_done, gram_ready, att_done, exp_done, tc_done, ca_done, x1_done, scaled_done, last_x1_done,
         last_sum_done) = (
            sem("ynt_ready"), sem("ynt_done"), sem("gram_ready"), sem("att_done"), sem("exp_done"), sem("tc_done"),
            sem("ca_done"), sem("x1_done"), sem("scaled_done"), sem("last_x1_done"), sem("last_sum_done"))
        m2_ready, nm2_done, sq2_done, v2_ready, ve2_done, r2_done, nmr2_done, xn_done = (
            sem("m2_ready"), sem("nm2_done"), sem("sq2_done"), sem("v2_ready"), sem("ve2_done"), sem("r2_done"),
            sem("nmr2_done"), sem("xn_done"))
        passed_pool, passed_pe = sem("passed_pool"), sem("passed_pe")
        gv, yq, rdone = sem("gate_var_step"), sem("pooled_norm_step"), sem("recip_done")
        xt_ready, xt_copied, mix_ready, added, placed = (
            sem("xt_ready"), sem("xt_copied"), sem("mix_ready"), sem("added"), sem("placed"))

        block = ctx.enter_context(nc.Block())

        TAPS2 = 2 * NTAPS
        ATT = 7
        XN = 6
        FD = 3
        HB = 3
        BACK = UNITS * T

        def freed(n, k, places):
            return (n - 1) * BACK + (k - places + 1 if k >= places else 0)

        def in_place(eng, n, units):
            for s, own in ((added, ADDED), (placed, PLACED)):
                last = max([own.index(k) for k in units if k in own], default=None)
                if last is not None:
                    wait(eng, s, (n - 1) * len(own) + last + 1)

        def wait(eng, s, value):
            if not (isinstance(value, int) and value <= 0):
                eng.wait_ge(s, value)

        def image(ap):
            return ap.rearrange("p (h w) -> p h w", w=W)

        def kind_of(j):
            return INTERIOR if j < COLS else (SIDES if j == COLS else ENDS)

        def image_pieces(t_map):
            m = image(t_map)
            ends = m.rearrange("p (e r) w -> p e r w", r=SHIFT)
            mid = m[:, SHIFT:SHIFT + IN, :]
            return ([mid[:, :, SHIFT:SHIFT + IN].rearrange("p h (k c) -> p k h c", c=WS),
                     mid.rearrange("p h (s c) -> p h s c", c=SHIFT)[:, :, 0:14:13, :]]
                    + [ends[:, 13 * e, :, SHIFT:SHIFT + IN].rearrange("p r (k c) -> p k r c", c=WS) for e in range(2)]
                    + [ends[:, 13 * e].rearrange("p r (s c) -> p r s c", c=SHIFT)[:, :, 0:14:13, :] for e in range(2)])

        def column(t_map, j):
            return image(t_map)[:, SHIFT:SHIFT + IN, SHIFT + WS * j:SHIFT + WS * (j + 1)]

        def sides_in(unit):
            return [unit[:, 0:NB3].rearrange("p (h s c) -> p h s c", s=2, c=SHIFT)]

        def ends_in(unit):
            e4 = unit[:, 0:NB3].rearrange("p (k e r c) -> p e k r c", e=2, r=SHIFT, c=WS)
            c4 = unit[:, NB3:NB3 + 64].rearrange("p (e r s c) -> p e r s c", e=2, r=SHIFT, s=2)
            return [e4[:, 0], e4[:, 1], c4[:, 0], c4[:, 1]]

        @block.sync
        def _(sp):
            for dst, src in ((ident[:, :], ident_d), (gmean[:, :], gmean_d)):
                sp.dma_start(dst, src).then_inc(matrices_in, 16)
            for t in range(T):
                sp.dma_start(xs[:, 0, t, :], x[0, t * P:(t + 1) * P, :]).then_inc(x_in[t], 16)
            for dst, src in ((wc[:, :, :], w_conv), (bc[:, :, :], b_conv), (gmb[:, :, :], gam)):
                sp.dma_start(dst, src).then_inc(consts_in, 16)
            for q in range(HPT):
                rows = slice(HD * q, HD * (q + 1))
                wk_v = wk.rearrange("(t q c) -> q t c", q=HPT, c=HD)[q:q + 1].broadcast_to([HD, T, HD])
                wv_v = wv.rearrange("(t q c) -> q t c", q=HPT, c=HD)[q:q + 1].broadcast_to([HD, T, HD])
                sp.dma_start(wqk_s[rows, :, :], wk_v).then_inc(consts_in, 16)
                sp.dma_start(wv_s[rows, :, :], wv_v).then_inc(consts_in, 16)
            sp.wait_ge(zeros_set, 1)
            for part in range(3):
                sp.dma_start(ub[32 * part:32 * part + HEADS, 0, 0:KINDS * P], b_win).then_inc(b_in, 16)
            sp.dma_start(ub[:, 1, 0:T * P], heads_d).then_inc(b_in, 16)
            sp.dma_start(wwin[:, :, :, :], w_win[:, 0:CORNERS]).then_inc(wwin_in, 16)
            sp.dma_start(wcor[:, :, :], w_win[0:2 * HD, CORNERS, :, 0:2 * HD]).then_inc(wwin_in, 16)
            for t in range(T):
                sp.wait_ge(x_in[t], 16)
                sp.dma_start(xs[:, 1, t, :], x[1, t * P:(t + 1) * P, :]).then_inc(x_in[t], 16)

            def load_next(n, par, t):
                sp.wait_ge(out_done[t], n * 16)
                sp.dma_start(xs[:, 1 - par, t, :], x[n + 1, t * P:(t + 1) * P, :]).then_inc(x_in[t], 16)

            def step(n, par, load):
                for t in range(T):
                    in_place(sp, n, [UNITS * t + UNITS - 1])
                    sp.dma_start(out[n - 1, t * P:(t + 1) * P, :], xs[:, 1 - par, t, :]).then_inc(out_done[t], 16)
                    if load:
                        load_next(n, par, t)

            step(1, 1, True)
            with sp.Fori(0, (B - 4) // 2) as it:
                step(it * 2 + 2, 0, True)
                step(it * 2 + 3, 1, True)
            step(B - 2, 0, True)
            step(B - 1, 1, False)
            step(B, 0, False)
            for t in range(T):
                sp.wait_ge(out_done[t], B * 16)

        @block.gpsimd
        def _(pool):
            pool.memset(ub[:, 0:2, 0:T * P], 0.0)
            pool.memset(xp[:, :, :, :], 0.0)
            pool.memset(eps_s[:, :], EPS)
            pool.memset(mhalf[:, :], -0.5)
            pool.memset(ones_h[:, :], 1.0 / (P * H))
            pool.memset(ones_l[:, :], 1.0).then_inc(zeros_set, 1)

            def rsqrt(dst, src, k):
                return nc.gpsimd.tensor_tensor(dst, src, mhalf[:, 0:k], ALU.pow)

            def last_out(par, half):
                c = slice(half * (HW // 2), (half + 1) * (HW // 2))
                nc.gpsimd.tensor_tensor(xs[:, par, T - 1, c], xs[:, par, T - 1, c], ub[:, T - 1, c], ALU.add)\
                    .then_inc(last_x1_done, 1)

            def normalise(n, par, t):
                c = slice(t, t + 1)
                pool.wait_ge(ve2_done, (n - 1) * T + t + 1)
                rsqrt(r2[:, c], ve2[:, c], 1).then_inc(r2_done, 1)
                pool.wait_ge(r2_done, (n - 1) * T + t + 1)
                nc.gpsimd.tensor_tensor(nmr2[:, c], nm2[:, c], r2[:, c], ALU.mult).then_inc(nmr2_done, 1)
                pool.wait_ge(nmr2_done, (n - 1) * T + t + 1)
                pool.sem_inc(passed_pool, 1)
                blocks = ub[:, t, :]
                forms = ([blocks[:, 0:COLS * NB3].rearrange("p (k h c) -> p k h c", k=COLS, c=WS)]
                         + sides_in(blocks[:, COLS * NB3:]) + ends_in(blocks[:, (COLS + 1) * NB3:]))
                for src, dst in zip(image_pieces(xs[:, 1 - par, t, :]), forms):
                    nc.gpsimd.tensor_scalar(dst, src, r2[:, c], nmr2[:, c], ALU.mult, ALU.add).then_inc(xn_done, 1)

            def step(n, par, front, back, ahead):
                if front:
                    pool.wait_ge(ve1_done, n + 1)
                    rsqrt(r1[:, :], ve1[:, :], T).then_inc(r1_done, 1)
                def rstd_of_conv(i, d):
                    pool.wait_ge(vh_done, 2 * n + i + 1)
                    rsqrt(rh[:, T * d:T * (d + 1)], hv[:, 2, T * d:T * (d + 1)], T).then_inc(rh_done, 1)

                if back:
                    normalise(n, par, 0)
                    normalise(n, par, 1)
                if front:
                    rstd_of_conv(0, 1)
                if back:
                    last_out(1 - par, 1)
                if front:
                    rstd_of_conv(1, 0)
                if back:
                    normalise(n, par, 2)
                    if not front:
                        normalise(n, par, 3)
                if not front:
                    return
                def fold_columns(m, mpar, t):
                    pool.wait_ge(x_in[t], (m + 1) * 16)
                    if t == 0:
                        pool.wait_ge(sq1_done, m * T)
                        if back:
                            pool.wait_ge(sq2_done, n * T)
                    else:
                        pool.wait_ge(rowsum_done, m * T + t)
                    pool.sem_inc(passed_pool, 1)
                    f = image(xs[:, mpar, t, :])
                    nc.gpsimd.tensor_tensor(fold, f[:, :, 0:W // 2], f[:, :, W // 2:W], ALU.add).then_inc(fold_done, 1)

                for t in range(T):
                    if t == T - 1:
                        pool.wait_ge(yvar_done, n + 1)
                        rsqrt(ry[:, :], yv[:, 1:2], 1).then_inc(ry_done, 1)
                    pool.wait_ge(wmax_done, n * T + t + 1)
                    m = image(ub[:, t, :])
                    g = th[:, 0, t, :].unsqueeze(2).broadcast_to([P, H, W])
                    nc.gpsimd.tensor_tensor(m, m, g, ALU.mult).then_inc(v_done, 1)
                    if ahead and t < FOLDED:
                        fold_columns(n + 1, 1 - par, t)
                    if back and t == 0:
                        normalise(n, par, 3)
                pool.wait_ge(ca_done, n + 1)
                pool.wait_ge(v_done, (n + 1) * T)
                pool.sem_inc(passed_pool, 1)
                last = ub[:, T - 1, :]
                nc.gpsimd.tensor_scalar(last, last, ca[:, T - 1:T], 0.0, ALU.mult, ALU.add).then_inc(scaled_done, 1)
                pool.wait_ge(scaled_done, n + 1)
                last_out(par, 0)

            step(0, 0, True, False, True)
            step(1, 1, True, True, True)
            with pool.Fori(0, (B - 4) // 2) as it:
                step(it * 2 + 2, 0, True, True, True)
                step(it * 2 + 3, 1, True, True, True)
            step(B - 2, 0, True, True, True)
            step(B - 1, 1, True, True, False)
            step(B, 0, False, True, False)

        @block.scalar
        def _(act):
            def evac(n, par, *units):
                for k in units:
                    wait(act, mix_ready, freed(n, k, XT_SLOTS))
                    act.wait_ge(xt_ready, (n - 1) * BACK + k + 1)
                    w = 4 * P if k % UNITS == UNITS - 1 else NB3
                    nc.scalar.activation(xt[:, k % XT_SLOTS, 0:w], p_xt[k % XP_BANKS][:, 0:w], ACT.Copy)\
                      .then_inc(xt_copied, 1)
                    if k - 2 in PLACED:
                        place(n, par, k - 2)

            def place(n, par, k):
                t, j = divmod(k, UNITS)
                act.wait_ge(mix_ready, (n - 1) * BACK + k + 1)
                nc.scalar.activation(column(xs[:, 1 - par, t, :], j),
                                     p_y[k % Y_BANKS][:, 0:NB3].rearrange("p (h c) -> p h c", c=WS), ACT.Copy)\
                  .then_inc(placed, 1)

            def group_mean(n, t):
                act.wait_ge(m1_ready, n * T + t + 1)
                nc.scalar.activation(nm1[:, t:t + 1], p_m1[:, t:t + 1], ACT.Copy, scale=-1.0).then_inc(nm1_done, 1)

            def square1(n, par, t):
                act.wait_ge(x_in[t], (n + 1) * 16)
                act.wait_ge(nm1_done, n * T + t + 1)
                nc.scalar.activation(junk, xs[:, par, t, :], ACT.Square, bias=nm1[:, t:t + 1],
                                     accum_out=sq1[:, t:t + 1]).then_inc(sq1_done, 1)

            def var1(n):
                act.wait_ge(v1_ready, n + 1)
                nc.scalar.activation(ve1[:, :], p_v1, ACT.Identity, bias=eps_s[:, :]).then_inc(ve1_done, 1)

            def group_mean2(n, t):
                act.wait_ge(m2_ready, (n - 1) * T + t + 1)
                nc.scalar.activation(nm2[:, t:t + 1], p_m2[:, t:t + 1], ACT.Copy, scale=-1.0).then_inc(nm2_done, 1)

            def last_sum(n, par):
                act.wait_ge(last_x1_done, 2 * n)
                nc.scalar.activation(junk, xs[:, 1 - par, T - 1, :], ACT.Copy, accum_out=s2[:, T - 1:T])\
                    .then_inc(last_sum_done, 1)

            def square2(n, par, t):
                act.wait_ge(nm2_done, (n - 1) * T + t + 1)
                nc.scalar.activation(junk, xs[:, 1 - par, t, :], ACT.Square, bias=nm2[:, t:t + 1],
                                     accum_out=sq2[:, t:t + 1]).then_inc(sq2_done, 1)

            def var2(n, t):
                act.wait_ge(v2_ready, (n - 1) * T + t + 1)
                nc.scalar.activation(ve2[:, t:t + 1], p_v2[:, t:t + 1], ACT.Identity, bias=eps_s[:, :])\
                    .then_inc(ve2_done, 1)

            def step(n, par, front, back, ahead):
                if back:
                    act.wait_ge(sq1_done, (n + 1) * T if front else n * T)
                    for t in range(T - 1):
                        if t > 0:
                            group_mean2(n, t)
                            var2(n, t - 1)
                            act.wait_ge(sq2_done, (n - 1) * T + t)
                        if t == 2:
                            evac(n, par, 0, 1)
                        square2(n, par, t)
                    evac(n, par, 2)
                    var2(n, T - 2)
                    evac(n, par, 3, 4)

                def conv_means(i, d):
                    act.wait_ge(fm_ready, 2 * n + i + 1)
                    c = slice(2 * T * d, 2 * T * (d + 1))
                    nc.scalar.activation(fm[:, c], p_fm[:, c], ACT.Copy).then_inc(fm_done, 1)

                def tanhs(i, d):
                    act.wait_ge(hb_done, HB * (2 * n + i + 1))
                    for t in range(T):
                        k = d * T + t
                        nc.scalar.activation(th[:, d, t, :], ff[:, 0, d, t, :], ACT.Tanh,
                                             scale=hv[:, 1, k:k + 1], bias=hv[:, 3, k:k + 1]).then_inc(th_done, 1)

                if front:
                    conv_means(0, 1)
                if back:
                    evac(n, par, 5, 6, 7)
                if front:
                    tanhs(0, 1)
                if back:
                    evac(n, par, 8, 9)
                if front:
                    conv_means(1, 0)
                if back:
                    evac(n, par, 10)
                    act.wait_ge(sq2_done, n * T - 1)
                    last_sum(n, par)
                    evac(n, par, 11)
                if front:
                    tanhs(1, 0)
                if back:
                    evac(n, par, 12, 13)
                    group_mean2(n, T - 1)
                    evac(n, par, 14)
                    act.wait_ge(last_sum_done, n)
                    square2(n, par, T - 1)
                    evac(n, par, 15, 16)
                    var2(n, T - 1)
                    evac(n, par, *range(17, BACK))
                if not front:
                    return
                m, mpar = n + 1, 1 - par
                if ahead:
                    group_mean(m, 0)
                    group_mean(m, 1)
                    act.wait_ge(rowsum_done, m * T + FOLDED)
                    square1(m, mpar, 0)
                act.wait_ge(ym_ready, n + 1)
                nc.scalar.activation(ym[:, :], p_ym, ACT.Copy, scale=float(P * H) / (C * L)).then_inc(ym_done, 1)
                if ahead:
                    act.wait_ge(sq1_done, m * T + 1)
                    square1(m, mpar, 1)
                    group_mean(m, 2)
                act.wait_ge(ynt_ready, n + 1)
                nc.scalar.activation(ynt, p_ynt, ACT.Copy).then_inc(ynt_done, 1)
                if ahead:
                    act.wait_ge(sq1_done, m * T + 2)
                    square1(m, mpar, 2)
                act.wait_ge(att_done, ATT * n + 3)
                nc.scalar.activation(ee[:, 0, :, :], at[:, :, :], ACT.Exp).then_inc(exp_done, 1)
                if ahead:
                    group_mean(m, 3)
                act.wait_ge(att_done, ATT * n + 7)
                nc.scalar.activation(tc[:, :], oo[:, :], ACT.Tanh, scale=0.5).then_inc(tc_done, 1)
                if ahead:
                    act.wait_ge(sq1_done, m * T + 3)
                    square1(m, mpar, 3)
                group_mean2(m, 0)
                if ahead:
                    var1(m)

            act.wait_ge(zeros_set, 1)
            act.wait_ge(psum_clear, 1)
            for t in range(T):
                group_mean(0, t)
                wait(act, sq1_done, t)
                square1(0, 0, t)
            var1(0)
            step(0, 0, True, False, True)
            step(1, 1, True, True, True)
            with act.Fori(0, (B - 4) // 2) as it:
                step(it * 2 + 2, 0, True, True, True)
                step(it * 2 + 3, 1, True, True, True)
            step(B - 2, 0, True, True, True)
            step(B - 1, 1, True, True, False)
            step(B, 0, False, True, False)

        @block.tensor
        def _(pe):
            pe.wait_ge(psum_clear, 1)
            pe.wait_ge(matrices_in, 16 * 2)

            def colsum(n, par, t, part=None):
                groups = H // 4
                first, end = (0, groups) if part is None else ((0, groups // 2), (groups // 2, groups))[part]
                if first == 0:
                    pe.wait_ge(x_in[t], (n + 1) * 16)
                    if not (isinstance(n, int) and n < 2):
                        in_place(pe, n - 1, [BACK - T + t])
                v = xs[:, par, t, :].rearrange("p (g f) -> p g f", f=4 * W)
                for g in range(first, end):
                    mm = pe.matmul(p_col[t][:, 0:4 * W], ident[:, :], v[:, g, :],
                                   start=(g == 0), stop=(g == groups - 1))
                if end == groups:
                    mm.then_inc(colsum_ready, 1)

            def group_mean(n, t):
                pe.wait_ge(chsum_done, n * T + t + 1)
                wait(pe, nm1_done, n * T + t)
                wait(pe, ym_done, n if t > 1 else n - 1)
                pe.matmul(p_m1[:, t:t + 1], gmean[:, :], chs[:, t:t + 1], start=True, stop=True).then_inc(m1_ready, 1)

            def var1(n):
                pe.wait_ge(sq1_done, (n + 1) * T)
                pe.matmul(p_v1, gmean[:, :], sq1[:, :], start=True, stop=True).then_inc(v1_ready, 1)

            def mean(n, t):
                if t < T - 1:
                    pe.wait_ge(x1_done, (n - 1) * (T - 1) + t + 1)
                else:
                    pe.wait_ge(last_sum_done, n)
                wait(pe, nm2_done, (n - 1) * T + t)
                wait(pe, ve2_done, (n - 1) * T + (t if t == T - 1 else max(t - 1, 0)))
                pe.matmul(p_m2[:, t:t + 1], gmean[:, :], s2[:, t:t + 1], start=True, stop=True).then_inc(m2_ready, 1)

            def var(n, t):
                pe.wait_ge(sq2_done, (n - 1) * T + t + 1)
                pe.wait_ge(nm2_done, (n - 1) * T + (T if t == T - 1 else min(t + 2, T - 1)))
                wait(pe, ve2_done, (n - 1) * T + t)
                pe.matmul(p_v2[:, t:t + 1], gmean[:, :], sq2[:, t:t + 1], start=True, stop=True).then_inc(v2_ready, 1)

            def turn(n, k):
                t, j = divmod(k, UNITS)
                if j == 0:
                    pe.wait_ge(xn_done, (n - 1) * XN * T + XN * t + 1)
                if j >= COLS:
                    pe.wait_ge(xn_done, (n - 1) * XN * T + XN * t + (2 if j == COLS else XN))
                wait(pe, xt_copied, freed(n, k, XP_BANKS))
                if k < 2:
                    wait(pe, att_done, ATT * (n - 1) + 4)
                ps = p_xt[k % XP_BANKS]
                for b in range(3):
                    mm = pe.transpose(ps[:, b * P:(b + 1) * P], ub[:, t, j * NB3 + b * P:j * NB3 + (b + 1) * P],
                                      ident[:, :])
                if j == UNITS - 1:
                    mm = pe.transpose(ps[0:64, 3 * P:4 * P], ub[:, t, HW - 64:HW], ident[:, :])
                mm.then_inc(xt_ready, 1)

            def mix(n, par, k, front):
                t, j = divmod(k, UNITS)
                kind = kind_of(j)
                s = k % XT_SLOTS
                ps = p_y[k % Y_BANKS]
                if k >= Y_BANKS:
                    in_place(pe, n, [k - Y_BANKS])
                else:
                    in_place(pe, n - 1, [BACK - Y_BANKS + k])
                if front and k < T:
                    pe.wait_ge(colsum_read, n * T + k + 1)
                rhs = bpat[:, kind, :].unsqueeze(1).broadcast_to([P, 3, P])
                pe.matmul(ps[:, 0:NB3], heads[:, t, :], rhs, start=True, stop=False, skip_group_check=True)
                if j == UNITS - 1:
                    pe.matmul(ps[:, NB3:NB3 + 64], heads[:, t, :], bpat[:, CORNERS, 0:64], start=False, stop=False,
                              skip_group_check=True)
                pe.wait_ge(xt_copied, (n - 1) * BACK + k + 1)
                if k in PLACED:
                    pe.matmul(ps[:, 0:NB3], ident[:, :], column(xs[:, 1 - par, t, :], j), start=False, stop=False,
                              skip_group_check=True)
                nb = 4 if j == UNITS - 1 else 3
                for b in range(nb):
                    for q in range(HPT):
                        rows = slice(HD * q, HD * (q + 1))
                        cols = slice(b * P + HD * q, b * P + HD * (q + 1))
                        if b == 3:
                            o, xb, wb = ps[rows, NB3:NB3 + 64], xt[0:64, s, cols], wcor[:, t * HPT + q, :]
                        else:
                            o, xb, wb = ps[rows, b * P:(b + 1) * P], xt[:, s, cols], wwin[:, kind, t * HPT + q, :]
                        mm = pe.matmul(o, xb, wb, start=False, stop=(b == nb - 1), skip_group_check=True,
                                       tile_position=(0, HD * q))
                mm.then_inc(mix_ready, 1)

            def step(n, par, front, back, ahead):
                if back:
                    mean(n, 2)
                    var(n, 1)
                    turn(n, 0)
                for k in range(BACK):
                    if back:
                        if k < BACK - 1:
                            turn(n, k + 1)
                        mix(n, par, k, front)
                        if k == 1:
                            var(n, 2)
                        if k == 12:
                            mean(n, 3)
                    if front and k in (3, 8):
                        i, c = ((0, slice(2 * T, 4 * T)) if k == 3 else (1, slice(0, 2 * T)))
                        pe.wait_ge(fstat_done, 2 * n + i + 1)
                        if i == 1:
                            pe.wait_ge(fm_done, 2 * n + 1)
                        pe.matmul(p_fm[:, c], ones_h[:, :], fs[:, c], start=True, stop=True).then_inc(fm_ready, 1)
                    if back and k == 15:
                        var(n, 3)
                if not front:
                    return
                m, mpar = n + 1, 1 - par
                if ahead:
                    group_mean(m, 0)
                    colsum(m, mpar, 0)
                    group_mean(m, 1)
                    colsum(m, mpar, 1, 0)
                    pe.wait_ge(nm1_done, m * T + 2)
                pe.wait_ge(ystat_done, n + 1)
                pe.matmul(p_ym, ones_h[:, :], ys[:, :], start=True, stop=True).then_inc(ym_ready, 1)
                if ahead:
                    colsum(m, mpar, 1, 1)
                    colsum(m, mpar, 2, 0)
                    group_mean(m, 2)
                wait(pe, xt_copied, n * BACK)
                pe.wait_ge(yn_done, T * (n + 1))
                pe.sem_inc(passed_pe, 1)
                for t in range(T):
                    mm = pe.transpose(p_ynt[:, t * P:(t + 1) * P], y[:, t, :], ident[:, :])
                mm.then_inc(ynt_ready, 1)
                pe.wait_ge(ynt_done, n + 1)
                pe.sem_inc(passed_pe, 1)
                for t in range(T):
                    for q in range(HPT):
                        rows = slice(HD * q, HD * (q + 1))
                        cols = slice(t * P + HD * q, t * P + HD * (q + 1))
                        pe.matmul(p_gram[rows, HD * t:HD * (t + 1)], ynt[:, cols], ynt[:, cols],
                                  start=True, stop=True, tile_position=(0, HD * q))
                for q in range(HPT):
                    rows = slice(HD * q, HD * (q + 1))
                    v = ynt.rearrange("p (t q c) -> p t q c", t=T, q=HPT)[:, :, q, :]
                    mm = pe.matmul(p_vb[rows, :], ones_l[:, :], v, start=True, stop=True, tile_position=(0, HD * q))
                mm.then_inc(gram_ready, 1)
                if ahead:
                    group_mean(m, 3)
                    colsum(m, mpar, 2, 1)
                mean(m, 0)
                if ahead:
                    var1(m)
                    colsum(m, mpar, 3, 0)
                mean(m, 1)
                var(m, 0)
                if ahead:
                    colsum(m, mpar, 3, 1)

            for t in range(T):
                colsum(0, 0, t)
                group_mean(0, t)
            var1(0)
            pe.wait_ge(zeros_set, 1)
            step(0, 0, True, False, True)
            pe.wait_ge(consts_set, 1)
            pe.wait_ge(wwin_in, 32)
            step(1, 1, True, True, True)
            with pe.Fori(0, (B - 4) // 2) as it:
                step(it * 2 + 2, 0, True, True, True)
                step(it * 2 + 3, 1, True, True, True)
            step(B - 2, 0, True, True, True)
            step(B - 1, 1, True, True, False)
            step(B, 0, False, True, False)

        @block.vector
        def _(dve):
            v = nc.vector
            for ps in p_xt + p_y + [p_front, p_back]:
                last = v.memset(ps[:, :], 0.0)
            last.then_inc(psum_clear, 1)
            def bcast(ap, w):
                return ap.unsqueeze(2).broadcast_to([P, ap.shape[1], w])

            def set_constants():
                dve.wait_ge(zeros_set, 1)
                dve.wait_ge(b_in, 16 * 4)
                v.memset(bpat[:, :, :], 0.0).then_inc(split, 1)
                v.tensor_copy(heads[:, :, :].rearrange("p t c -> p (t c)"), ub[:, 1, 0:T * P])
                bsrc = ub[:, 0, 0:KINDS * P]
                part = xt[:, 1, :].bitcast(BF16)[:, 0:KINDS * P]
                dve.wait_ge(split, 1)
                done = 1
                for k in range(3):
                    v.tensor_copy(part, bsrc).then_inc(split, 1)
                    done += 1
                    dve.wait_ge(split, done)
                    v.tensor_copy(bpat[32 * k:32 * (k + 1), :, :].rearrange("p k c -> p (k c)"),
                                  part[32 * k:32 * (k + 1), :])
                    v.tensor_tensor(bsrc, bsrc, part, ALU.subtract).then_inc(split, 1)
                    done += 1
                    dve.wait_ge(split, done)
                dve.wait_ge(consts_in, 16 * (3 + 2 * HPT))
                for t in range(T):
                    v.tensor_scalar(wqk_s[:, t, :], wqk_s[:, t, :], gmb[:, 6, t:t + 1], float(HD) ** -0.5,
                                    ALU.mult, ALU.mult)
                v.tensor_scalar(wv_s[:, :, :], wv_s[:, :, :], 1.0 / L, None, ALU.mult)
                v.tensor_scalar(gmb[:, 0:4, :], gmb[:, 0:4, :], 0.5, None, ALU.mult).then_inc(consts_set, 1)
                dve.wait_ge(consts_set, 1)

            def add_units(n, par, *units):
                for k in units:
                    if k in PLACED:
                        continue
                    t, j = divmod(k, UNITS)
                    ps = p_y[k % Y_BANKS]
                    dve.wait_ge(mix_ready, (n - 1) * BACK + k + 1)
                    if j < COLS:
                        pairs = [(column(xs[:, 1 - par, t, :], j), ps[:, 0:NB3].rearrange("p (h c) -> p h c", c=WS))]
                    else:
                        im = image_pieces(xs[:, 1 - par, t, :])
                        pairs = zip(im[1:2], sides_in(ps)) if j == COLS else zip(im[2:], ends_in(ps))
                    for m, product in pairs:
                        ins = v.tensor_tensor(m, product, m, ALU.add)
                    ins.then_inc(added, 1)

            def rowsum(n, par, t):
                if t < FOLDED and not (isinstance(n, int) and n == 0):
                    dve.wait_ge(fold_done, (n - 1) * FOLDED + t + 1)
                    src = fold
                else:
                    dve.wait_ge(x_in[t], (n + 1) * 16)
                    src = image(xs[:, par, t, :])
                v.tensor_reduce(rs[:, 0, t, :], src, AX.X, ALU.add).then_inc(rowsum_done, 1)

            def colsum_read_out(n, t):
                dve.wait_ge(colsum_ready, n * T + t + 1)
                v.tensor_reduce(rs[:, 1, t, :], p_col[t][:, 0:4 * W].rearrange("p (f w) -> p w f", w=W),
                                AX.X, ALU.add).then_inc(colsum_read, 1)

            def channel_sum(n, t):
                dve.wait_ge(rowsum_done, n * T + t + 1)
                v.tensor_reduce(chs[:, t:t + 1], rs[:, 0, t, :], AX.X, ALU.add).then_inc(chsum_done, 1)

            def centre(n):
                dve.wait_ge(nm1_done, (n + 1) * T)
                dve.wait_ge(colsum_read, (n + 1) * T)
                for d in range(2):
                    v.scalar_tensor_tensor(xp[:, d, :, PAD:PAD + H], bcast(nm1[:, :], H), float(H), rs[:, d, :, :],
                                           ALU.mult, ALU.add).then_inc(centred, 1)
                dve.wait_ge(centred, 2 * (n + 1))

            def convs(n, i, d, between):
                count, last = NTAPS * i, {}
                for tap in range(max(KS)):
                    for t in range(T):
                        if tap >= KS[t]:
                            continue
                        src = xp[:, d, t, PAD + tap - KS[t] // 2:PAD + tap - KS[t] // 2 + H]
                        wi = sum(KS[:t]) + tap
                        dst = ff[:, 0, d, t, :]
                        if tap == 0:
                            ins = v.tensor_scalar(dst, src, wc[:, d, wi:wi + 1], None, ALU.mult)
                        else:
                            dve.wait_ge(tap_done, TAPS2 * n + last[t])
                            ins = v.scalar_tensor_tensor(dst, src, wc[:, d, wi:wi + 1], dst, ALU.mult, ALU.add)
                        ins.then_inc(tap_done, 1)
                        count += 1
                        last[t] = count
                    if tap in between:
                        between[tap]()
                assert count == NTAPS * (i + 1)

            def conv_stats(n, i, d):
                f, sq = ff[:, 0, d, :, :], ff[:, 1, d, :, :]
                done = FD * (2 * n + i)
                if i == 0:
                    dve.wait_ge(r1_done, n + 1)
                dve.wait_ge(tap_done, TAPS2 * n + NTAPS * (i + 1))
                v.scalar_tensor_tensor(f, f, 1.0 / H, bcast(r1[:, :], H), ALU.mult, ALU.mult).then_inc(f_done, 1)
                dve.wait_ge(f_done, done + 1)
                v.tensor_tensor(f, f, bcast(bc[:, d, :], H), ALU.add).then_inc(f_done, 1)
                dve.wait_ge(f_done, done + 2)
                v.tensor_tensor(sq, f, f, ALU.mult).then_inc(f_done, 1)
                dve.wait_ge(f_done, done + 3)
                v.tensor_reduce(fs[:, 2 * T * d:2 * T * (d + 1)].rearrange("p (a t) -> p a t", a=2), ff[:, :, d, :, :],
                                AX.X, ALU.add).then_inc(fstat_done, 1)

            def gate_var(n, i, d):
                c = slice(T * d, T * (d + 1))
                mean, square = fm[:, 2 * T * d:2 * T * d + T], fm[:, 2 * T * d + T:2 * T * (d + 1)]
                dve.wait_ge(fm_done, 2 * n + i + 1)
                v.tensor_tensor(hv[:, 0, c], mean, mean, ALU.mult).then_inc(gv, 1)
                dve.wait_ge(gv, 4 * n + 2 * i + 1)
                v.tensor_tensor(hv[:, 0, c], square, hv[:, 0, c], ALU.subtract).then_inc(gv, 1)
                dve.wait_ge(gv, 4 * n + 2 * i + 2)
                v.tensor_scalar(hv[:, 2, c], hv[:, 0, c], 0.0, EPS, ALU.max, ALU.add).then_inc(vh_done, 1)

            def gate_affine(n, i, d):
                c = slice(T * d, T * (d + 1))
                done = HB * (2 * n + i)
                dve.wait_ge(rh_done, 2 * n + i + 1)
                v.tensor_tensor(hv[:, 1, c], rh[:, c], gmb[:, d, :], ALU.mult).then_inc(hb_done, 1)
                dve.wait_ge(hb_done, done + 1)
                v.tensor_tensor(hv[:, 3, c], fm[:, 2 * T * d:2 * T * d + T], hv[:, 1, c], ALU.mult).then_inc(hb_done, 1)
                dve.wait_ge(hb_done, done + 2)
                v.tensor_tensor(hv[:, 3, c], gmb[:, 2 + d, :], hv[:, 3, c], ALU.subtract).then_inc(hb_done, 1)

            def column_gate(n):
                dve.wait_ge(th_done, 2 * T * n + T)
                v.tensor_scalar(th[:, 1, :, :], th[:, 1, :, :], 0.25, 0.25, ALU.mult, ALU.add).then_inc(gate_done, 1)

            def row_gate(n):
                dve.wait_ge(th_done, 2 * T * (n + 1))
                v.scalar_tensor_tensor(th[:, 0, :, :], th[:, 0, :, :], 1.0, bcast(r1[:, :], H), ALU.add, ALU.mult)\
                 .then_inc(gate_done, 1)

            def gate_columns(n, par, t):
                if not (isinstance(n, int) and n == 0):
                    dve.wait_ge(xt_ready, (n - 1) * BACK + UNITS * (t + 1))
                g = th[:, 1, t, :].unsqueeze(1).broadcast_to([P, H, W])
                v.scalar_tensor_tensor(image(ub[:, t, :]), image(xs[:, par, t, :]), nm1[:, t:t + 1], g,
                                       ALU.add, ALU.mult).then_inc(u_done, 1)

            def pool_columns(n, t):
                dve.wait_ge(u_done, n * T + t + 1)
                wait(dve, y_done, n * T + t)
                v.tensor_reduce(pm[:, :], ub[:, t, :].rearrange("p (k w) -> p k w", w=WIN), AX.X, ALU.max)\
                 .then_inc(wmax_done, 1)

            def pool_rows(n, par, t, *between):
                q3 = pm[:, :].rearrange("p (h k) -> p h k", k=NW)
                dve.wait_ge(wmax_done, n * T + t + 1)
                if t == 0:
                    dve.wait_ge(gate_done, 2 * (n + 1))
                v.tensor_tensor(q3, q3, bcast(th[:, 0, t, :], NW), ALU.mult).then_inc(wgate_done, 1)
                add_units(n, par, *between)
                dve.wait_ge(wgate_done, n * T + t + 1)
                v.tensor_reduce(y[:, t, :], pm[:, :].rearrange("p (a r k) -> p a k r", r=WIN, k=NW), AX.X, ALU.max)\
                 .then_inc(y_done, 1)

            def pooled_sums(n):
                dve.wait_ge(y_done, T * (n + 1))
                yf = y[:, :, :].rearrange("p t l -> p (t l)")
                v.tensor_reduce(ys[:, 0:1], yf, AX.X, ALU.add)
                v.scalar_tensor_tensor(yj, yf, 1.0, yf, ALU.mult, ALU.mult, accum_out=ys[:, 1:2])\
                 .then_inc(ystat_done, 1)

            def pooled_var(n):
                dve.wait_ge(ym_done, n + 1)
                v.tensor_tensor(yv[:, 0:1], ym[:, 0:1], ym[:, 0:1], ALU.mult).then_inc(yq, 1)
                dve.wait_ge(yq, 5 * n + 1)
                v.tensor_tensor(yv[:, 0:1], ym[:, 1:2], yv[:, 0:1], ALU.subtract).then_inc(yq, 1)
                dve.wait_ge(yq, 5 * n + 2)
                v.tensor_scalar(yv[:, 1:2], yv[:, 0:1], 0.0, EPS, ALU.max, ALU.add).then_inc(yvar_done, 1)

            def pooled_norm(n):
                dve.wait_ge(ry_done, n + 1)
                v.tensor_scalar(ab[:, 0, :], gmb[:, 4, :], ry[:, 0:1], None, ALU.mult).then_inc(yq, 1)
                dve.wait_ge(yq, 5 * n + 3)
                v.tensor_scalar(ab[:, 1, :], ab[:, 0, :], ym[:, 0:1], None, ALU.mult).then_inc(yq, 1)
                dve.wait_ge(yq, 5 * n + 4)
                v.tensor_tensor(ab[:, 2, :], gmb[:, 5, :], ab[:, 1, :], ALU.subtract).then_inc(yq, 1)
                dve.wait_ge(yq, 5 * n + 5)
                for t in range(T):
                    v.tensor_scalar(y[:, t, :], y[:, t, :], ab[:, 0, t:t + 1], ab[:, 2, t:t + 1],
                                    ALU.mult, ALU.add).then_inc(yn_done, 1)

            def logits(n):
                g = p_gram.rearrange("p (t c) -> p t c", t=T)
                vb = p_vb.rearrange("p (t c) -> p t c", t=T)
                dve.wait_ge(gram_ready, n + 1)
                v.tensor_tensor(at[:, :, :], g, wqk_s[:, :, :], ALU.mult).then_inc(att_done, 1)
                dve.wait_ge(att_done, ATT * n + 1)
                v.tensor_reduce(mx[:, :], at[:, :, :], AX.X, ALU.max).then_inc(att_done, 1)
                dve.wait_ge(att_done, ATT * n + 2)
                v.tensor_tensor(at[:, :, :], at[:, :, :], bcast(mx[:, :], HD), ALU.subtract).then_inc(att_done, 1)
                v.tensor_tensor(ee[:, 1, :, :], vb, wv_s[:, :, :], ALU.mult).then_inc(att_done, 1)

            def attend(n):
                dve.wait_ge(exp_done, n + 1)
                dve.wait_ge(att_done, ATT * n + 4)
                v.tensor_tensor(ee[:, 1, :, :], ee[:, 0, :, :], ee[:, 1, :, :], ALU.mult).then_inc(att_done, 1)
                dve.wait_ge(att_done, ATT * n + 5)
                v.tensor_reduce(ss[:, :, :].rearrange("p a t -> p (a t)"),
                                ee[:, :, :, :].rearrange("p a t c -> p (a t) c"), AX.X, ALU.add).then_inc(att_done, 1)
                dve.wait_ge(att_done, ATT * n + 6)
                v.reciprocal(rd[:, :], ss[:, 0, :]).then_inc(rdone, 1)
                dve.wait_ge(rdone, n + 1)
                v.tensor_tensor(oo[:, :], ss[:, 1, :], rd[:, :], ALU.mult).then_inc(att_done, 1)

            def channel_gate(n):
                dve.wait_ge(tc_done, n + 1)
                v.tensor_scalar(ca[:, :], tc[:, :], 0.5, 0.5, ALU.mult, ALU.add).then_inc(ca_done, 1)
                dve.wait_ge(ca_done, n + 1)

            def first_out(n, par, t):
                dve.wait_ge(v_done, n * T + t + 1)
                v.scalar_tensor_tensor(xs[:, par, t, :], ub[:, t, :], ca[:, t:t + 1], xs[:, par, t, :],
                                       ALU.mult, ALU.add, accum_out=s2[:, t:t + 1]).then_inc(x1_done, 1)

            def step(n, par, front, back, ahead):
                def units(*ks):
                    if back:
                        add_units(n, par, *ks)

                if not front:
                    units(*range(BACK))
                    return
                centre(n)
                convs(n, 0, 1, {5: lambda: units(0)})
                conv_stats(n, 0, 1)
                units(1)
                convs(n, 1, 0, {0: lambda: units(2), 2: lambda: units(3), 3: lambda: gate_var(n, 0, 1),
                                5: lambda: units(4)})
                gate_affine(n, 0, 1)
                units(5)
                conv_stats(n, 1, 0)
                units(6, 7)
                gate_var(n, 1, 0)
                column_gate(n)
                m, mpar = n + 1, 1 - par
                dve.wait_ge(gate_done, 2 * n + 1)

                def sums(t, *between):
                    if ahead:
                        rowsum(m, mpar, t)
                    units(*between)
                    if ahead:
                        channel_sum(m, t)

                def rows(t, *between):
                    pool_rows(n, par, t, *(between if back else ()))

                def column_sums(t):
                    if ahead:
                        colsum_read_out(m, t)

                gate_columns(n, par, 0)
                gate_affine(n, 1, 0)
                units(8, 9, 10)
                row_gate(n)
                pool_columns(n, 0)
                units(11, 12, 13)
                rows(0, 14)
                gate_columns(n, par, 1)
                units(15, 16, 17, 18)
                pool_columns(n, 1)
                units(19, 20)
                sums(0, 21)
                rows(1, 22)
                gate_columns(n, par, 2)
                units(23, 24)
                pool_columns(n, 2)
                units(25, 26)
                rows(2, 27)
                units(28)
                sums(1, 29)
                gate_columns(n, par, 3)
                units(30, 31)
                pool_columns(n, 3)
                rows(3)
                pooled_sums(n)
                column_sums(0)
                pooled_var(n)
                sums(2)
                pooled_norm(n)
                column_sums(1)
                sums(3)
                logits(n)
                attend(n)
                channel_gate(n)
                for t in range(T - 1):
                    first_out(n, par, t)
                    if t == 1:
                        column_sums(2)
                column_sums(3)

            for t in range(T):
                rowsum(0, 0, t)
                channel_sum(0, t)
                colsum_read_out(0, t)
            set_constants()
            step(0, 0, True, False, True)
            step(1, 1, True, True, True)
            with dve.Fori(0, (B - 4) // 2) as it:
                step(it * 2 + 2, 0, True, True, True)
                step(it * 2 + 3, 1, True, True, True)
            step(B - 2, 0, True, True, True)
            step(B - 1, 1, True, True, False)
            step(B, 0, False, True, False)


def window_weights(w):
    out = np.zeros((P, KINDS, HEADS, P), w.dtype)
    for kind in range(KINDS):
        places = block_positions(kind)
        for win in range(4):
            at = [p for p, (v, _) in enumerate(places) if v == win]
            if at:
                pos = [places[p][1] for p in at]
                out[np.array(at)[:, None], kind, :, np.array(at)[None, :]] = w[:, pos][:, :, pos].transpose(2, 1, 0)
    return out


def window_bias(b):
    out = np.zeros((HEADS, KINDS, P), b.dtype)
    for kind in range(KINDS):
        places = block_positions(kind)
        out[:, kind, :len(places)] = b[:, [pos for _, pos in places]]
    return out.reshape(HEADS, KINDS * P)


def shape_constants():
    ident = np.eye(P, dtype=np.float32)
    gmean = np.kron(np.eye(P // GROUP), np.full((GROUP, GROUP), 1.0 / (GROUP * HW))).astype(np.float32)
    heads = np.zeros((P, T, P), np.float32)
    for part in range(3):
        for head in range(HEADS):
            t, q = divmod(head, HPT)
            heads[32 * part + head, t, HD * q:HD * (q + 1)] = 1.0
    return ident, gmean, heads.reshape(P, T * P)


def kernel(**inputs):
    import concourse.bacc as bacc
    from concourse.bass_utils import run_bass_kernel_spmd as run

    a = {k: np.asarray(v) for k, v in inputs.items()}
    g = {k[len("L0_conv_"):]: v for k, v in a.items() if k.startswith("L0_conv_")}

    def per_tile(names):
        return np.concatenate([g[k].reshape(P, -1) for k in names], axis=1)

    hs, ws = ("lh", "sh", "mh", "gh"), ("lw", "sw", "mw", "gw")
    ident, gmean, heads = shape_constants()
    arrays = {
        "x": np.ascontiguousarray(a["x"]).reshape(B, C, HW),
        "w_conv": np.ascontiguousarray(
            np.stack([per_tile(["w_" + k for k in hs]), per_tile(["w_" + k for k in ws])], 1)),
        "b_conv": np.ascontiguousarray(
            np.stack([per_tile(["b_" + k for k in hs]), per_tile(["b_" + k for k in ws])], 1)),
        "gam": np.ascontiguousarray(np.stack([g[k].reshape(T, P).T for k in (
            "gn_h_g", "gn_w_g", "gn_h_b", "gn_w_b", "gn_g", "gn_b", "wq")], 1)),
        "wk": np.ascontiguousarray(g["wk"]),
        "wv": np.ascontiguousarray(g["wv"]),
        "w_win": window_weights(a["L1_conv_w"]),
        "b_win": window_bias(a["L1_conv_b"]),
        "ident": ident,
        "gmean": gmean,
        "heads": heads,
    }
    nc = bacc.Bacc("TRN2", target_bir_lowering=False, num_devices=1)
    args = [nc.dram_tensor(k + "_in", v.shape, mybir.dt.from_np(v.dtype), kind="ExternalInput").ap()
            for k, v in arrays.items()]
    out = nc.dram_tensor("out", (B, C, HW), F32, kind="ExternalOutput").ap()
    build(nc, *args, out)
    got = run(nc, [{k + "_in": v for k, v in arrays.items()}], core_ids=[0]).results[0]["out"]
    return got.reshape(B, C, H, W)
```
